# Optimizing a Trainium2 kernel written in Bass

```python
import numpy as np
import jax
import jax.numpy as jnp

def _softmax(x, axis=-1):
    return jax.nn.softmax(x, axis=axis)

def _gelu(x):
    return jax.nn.gelu(x, approximate=True)

def _silu(x):
    return jax.nn.silu(x)

def _sigmoid(x):
    return jax.nn.sigmoid(x)

def _layernorm(x, axis=-1, eps=1e-05):
    m = jnp.mean(x, axis=axis, keepdims=True)
    v = jnp.var(x, axis=axis, keepdims=True)
    return (x - m) / jnp.sqrt(v + eps)

def _scatter_add(tgt, idx, src, axis=0):
    return tgt.at[idx].add(src)

def _segment_sum(src, seg, n):
    return jax.ops.segment_sum(src, seg, n)
kernel_name = 'mk_cond_resid_d2_seqx_r4_352840'

def setup_inputs(seed: int=0):
    np.random.seed(seed)
    _w = jnp.asarray

    def _rec_inputs():
        import jax
        import jax.numpy as jnp
        _rk = jax.random.key(seed)
        x = 8.748e-05 + 1 * jax.random.normal(jax.random.fold_in(_rk, 1), (4, 512, 512), jnp.float32)
        _lenS = 512 - jax.random.randint(jax.random.fold_in(_rk, 7), (4,), 0, max(1, 512 // 4) + 1, jnp.int32)
        _lenS2 = 512 - jax.random.randint(jax.random.fold_in(_rk, 8), (4,), 0, max(1, 512 // 4) + 1, jnp.int32)
        fside_BxSx1_0 = -0.00499425 + 1.0058 * jax.random.normal(jax.random.fold_in(_rk, 11), (4, 512, 1), jnp.float32)
        cond_2048 = 0.00513981 + 1.0024 * jax.random.normal(jax.random.fold_in(_rk, 12), (4, 512), jnp.float32)
        return (x, fside_BxSx1_0, cond_2048)
    x, fside_BxSx1_0, cond_2048 = _rec_inputs()

    def _L0_cond_setup():
        import jax, jax.numpy as jnp
        import numpy as np
        G, N, K = (16, 512, 5120)
        key = jax.random.key(seed)
        k1, k2, k3 = jax.random.split(key, 3)
        return {'emb_s': jax.random.normal(k1, (G, N, 1), dtype=jnp.float32), 'emb_t': jax.random.normal(k2, (G, 1, N), dtype=jnp.float32), 'attention_weights': jax.random.normal(k3, (G, N, N), dtype=jnp.float32), 'k': K}
    _L0_cond_all = _L0_cond_setup()
    _L0_cond_in = {k: v for k, v in _L0_cond_all.items() if k in ()}
    del _L0_cond_all

    def _L1_cond_setup():
        import jax, jax.numpy as jnp
        import numpy as np
        DIM = 512
        H = 16
        DH = 128
        INNER = H * DH
        MLP = 4 * DIM
        B, T = (2, 512)
        EPS = 1e-06

        def _ln(x):
            mu = jnp.mean(x, axis=-1, keepdims=True)
            var = jnp.var(x, axis=-1, keepdims=True)
            return (x - mu) * jax.lax.rsqrt(var + EPS)
        key = jax.random.key(seed)
        ks = jax.random.split(key, 12)
        s = 0.02
        return {'x': jax.random.normal(ks[0], (B, T, DIM), jnp.float32), 'timestep_embed': jax.random.normal(ks[1], (B, DIM), jnp.float32), 'ada_w': jax.random.normal(ks[2], (DIM, 6 * DIM), jnp.float32) * s, 'ada_b': jnp.zeros((6 * DIM,), jnp.float32), 'qkv_w': jax.random.normal(ks[3], (DIM, 3 * INNER), jnp.float32) * s, 'qkv_b': jnp.zeros((3 * INNER,), jnp.float32), 'out_w': jax.random.normal(ks[4], (INNER, DIM), jnp.float32) * s, 'out_b': jnp.zeros((DIM,), jnp.float32), 'ffn_w1': jax.random.normal(ks[5], (DIM, MLP), jnp.float32) * s, 'ffn_b1': jnp.zeros((MLP,), jnp.float32), 'ffn_w2': jax.random.normal(ks[6], (MLP, DIM), jnp.float32) * s, 'ffn_b2': jnp.zeros((DIM,), jnp.float32)}
    _L1_cond_all = _L1_cond_setup()
    _L1_cond_in = {k: v for k, v in _L1_cond_all.items() if k in ('ada_w', 'ada_b', 'qkv_w', 'qkv_b', 'out_w', 'out_b', 'ffn_w1', 'ffn_b1', 'ffn_w2', 'ffn_b2')}
    del _L1_cond_all
    return {'x': x, 'fside_BxSx1_0': fside_BxSx1_0, 'cond_2048': cond_2048, 'L1_cond_ada_w': _L1_cond_in['ada_w'], 'L1_cond_ada_b': _L1_cond_in['ada_b'], 'L1_cond_qkv_w': _L1_cond_in['qkv_w'], 'L1_cond_qkv_b': _L1_cond_in['qkv_b'], 'L1_cond_out_w': _L1_cond_in['out_w'], 'L1_cond_out_b': _L1_cond_in['out_b'], 'L1_cond_ffn_w1': _L1_cond_in['ffn_w1'], 'L1_cond_ffn_b1': _L1_cond_in['ffn_b1'], 'L1_cond_ffn_w2': _L1_cond_in['ffn_w2'], 'L1_cond_ffn_b2': _L1_cond_in['ffn_b2']}

def reference(x, fside_BxSx1_0, cond_2048, L1_cond_ada_w, L1_cond_ada_b, L1_cond_qkv_w, L1_cond_qkv_b, L1_cond_out_w, L1_cond_out_b, L1_cond_ffn_w1, L1_cond_ffn_b1, L1_cond_ffn_w2, L1_cond_ffn_b2):
    import jax
    import jax.numpy as jnp

    def _L0_cond_ref(emb_s, emb_t, attention_weights, k):
        import jax, jax.numpy as jnp
        import numpy as np
        G, N, K = (16, 512, 5120)
        g, n = (emb_s.shape[0], emb_s.shape[1])
        adj = emb_s * emb_t
        att = jax.nn.softmax(attention_weights, axis=-1) * (1.0 / np.sqrt(n).astype(np.float32))
        adj = adj * att
        diag = jnp.arange(n)
        adj = adj.at[:, diag, diag].set(-jnp.inf)
        flat = adj.reshape(g, n * n)
        _, idx = jax.lax.top_k(flat, k)
        rows = jnp.arange(g)[:, None]
        out = jnp.zeros((g, n * n), dtype=adj.dtype).at[rows, idx].set(1.0)
        return out.reshape(g, n, n)

    def _L1_cond_ref(x, timestep_embed, ada_w, ada_b, qkv_w, qkv_b, out_w, out_b, ffn_w1, ffn_b1, ffn_w2, ffn_b2):
        import jax, jax.numpy as jnp
        import numpy as np
        DIM = 512
        H = 16
        DH = 128
        INNER = H * DH
        MLP = 4 * DIM
        B, T = (2, 512)
        EPS = 1e-06

        def _ln(x):
            mu = jnp.mean(x, axis=-1, keepdims=True)
            var = jnp.var(x, axis=-1, keepdims=True)
            return (x - mu) * jax.lax.rsqrt(var + EPS)
        Bc, Tc, D = x.shape
        ada = (timestep_embed @ ada_w + ada_b)[:, None, :]
        shift1, scale1, gate1, shift2, scale2, gate2 = jnp.split(ada, 6, axis=-1)
        x1 = _ln(x) * (1.0 + scale1) + shift1
        qkv = (x1 @ qkv_w + qkv_b).reshape(Bc, Tc, 3, H, DH)
        q, k, v = (qkv[:, :, 0], qkv[:, :, 1], qkv[:, :, 2])
        scale = DH ** (-0.5)
        attn = jnp.einsum('bthd,bshd->bhts', q, k) * scale
        attn = jax.nn.softmax(attn, axis=-1)
        attn_out = jnp.einsum('bhts,bshd->bthd', attn, v).reshape(Bc, Tc, INNER)
        attn_out = attn_out @ out_w + out_b
        x = x + gate1 * attn_out
        x2 = _ln(x) * (1.0 + scale2) + shift2
        h = jax.nn.gelu(x2 @ ffn_w1 + ffn_b1, approximate=False)
        x = x + gate2 * (h @ ffn_w2 + ffn_b2)
        return x
    x = x + _L0_cond_ref(fside_BxSx1_0, cond_2048[:, None, :], x, 5120)
    x = x + _L1_cond_ref(x, cond_2048, L1_cond_ada_w, L1_cond_ada_b, L1_cond_qkv_w, L1_cond_qkv_b, L1_cond_out_w, L1_cond_out_b, L1_cond_ffn_w1, L1_cond_ffn_b1, L1_cond_ffn_w2, L1_cond_ffn_b2)
    return x

_drawn_inputs = setup_inputs


def setup_inputs(seed=0):
    import zlib

    import numpy as np

    out = dict(_drawn_inputs(seed))
    spreads = {'L1_cond_ada_b': (0.0, 0.363),
     'L1_cond_qkv_b': (0.0, 0.385),
     'L1_cond_out_b': (0.0, 0.359),
     'L1_cond_ffn_b1': (0.0, 0.672),
     'L1_cond_ffn_b2': (0.0, 0.361)}
    factors = {}
    for name, (base, spread) in spreads.items():
        noise = np.random.default_rng([zlib.crc32(name.encode()), seed]).standard_normal(out[name].shape)
        drawn = base * np.exp(spread * noise) if base else spread * noise
        out[name] = jnp.asarray(drawn.astype(out[name].dtype))
    for name, factor in factors.items():
        out[name] = (out[name] * factor).astype(out[name].dtype)
    return out
```

```python
from contextlib import ExitStack

import numpy as np

import concourse.bass as bass
from concourse import mybir

F32 = mybir.dt.float32
F32R = mybir.dt.float32r
I32 = mybir.dt.int32
U16 = mybir.dt.uint16
BF16 = mybir.dt.bfloat16
ALU = mybir.AluOpType
ACT = mybir.ActivationFunctionType
AX = mybir.AxisListType

P = 128
B, T, D = 4, 512, 512
H, DH = 16, 128
F = 2048
KTOP = 5120
EPS = 1e-6
SCALE = DH ** -0.5
C = D // P
NT = T // P
KC = F // P
HALF = 1024
QUAD = 4
NHALF = 48
NQKV = 24
NUNIT = 12
STEPS = 32
LEVEL = 16
NCOUNT = T * T // P // 2
TOP_BIT = float(1 << (LEVEL - 1))

COLS = {}
_at = 0
for _name, _n in (("bq", H), ("bk", H), ("bv", H), ("ob", C), ("b1", KC), ("b2", C),
                  ("ada_b", 6 * C), ("s", B * NT), ("cond", C * B)):
    COLS[_name] = (_at, _at + _n)
    _at += _n
NCOLS = _at


def bisection_slots():
    places = [("out", u, r) for u in range(1, 4) for r in range(4)]
    places += [(ph, u, r) for ph in ("mlp_in", "mlp_out") for u in range(4) for r in range(4)]
    del places[LEVEL]
    return {place: step for step, place in enumerate(places[:STEPS])}


SLOTS = bisection_slots()
RANK_SLOT = ("mlp_out", 1, 3)
LN1_SLOT = ("mlp_out", 3, 2)


def v_half(q, j):
    return j if q == 0 else 4 + 6 * (q - 1) + j


def qk_half(h):
    if h < 2:
        return 2 + h
    if h < 14:
        return 4 + 6 * ((h - 2) // 4) + 2 + (h - 2) % 4
    return 22 + h - 14


def block_kernel(nc, x, cond, weights, ada_w, cols, out):
    ctx = ExitStack()
    with ctx:
        here = [(nc.sbuf_base + 31) // 32 * 32]

        def at(name, shape, dt, offset):
            return nc.alloc_sbuf_tensor_at(name, shape, dt, offset=offset)

        def room(nbytes):
            offset = here[0]
            here[0] += (nbytes + 31) // 32 * 32
            assert here[0] <= nc.sbuf_usable_end, here[0]
            return offset

        def new(name, shape, dt):
            n = 4 if dt in (F32, F32R, I32) else 2
            for s in shape[1:]:
                n *= s
            return at(name, shape, dt, room(n))

        xm = new("xm", [P, NT, D], F32)
        xn = new("xn", [P, NT, D], F32)
        xT = new("xT", [P, 2, C, T], F32R)
        wraw = new("wraw", [P, 2, HALF], F32)
        w = new("w", [P, 2, 2, 2 * HALF], F32R)
        qk = new("qk", [P, 2, 2, T], F32R)
        act_at = room(2 * KC * T * 4)
        act = at("act", [P, 2, KC, T], F32R, act_at)
        adaw = at("adaw", [P, C, 6 * D], F32, act_at)
        prob = new("prob", [P, NT, T], F32)
        rank = prob[:, :, :].rearrange("p i d -> p (i d)")
        keys = rank.bitcast(I32)
        keys16 = rank.bitcast(U16).rearrange("p (n s) -> p n s", s=2)
        pt_at = room(2 * NT * T * 4)
        probT = at("probT", [P, 2, NT, T], F32R, pt_at)
        flip = at("flip", [P, NT * T], I32, pt_at)
        low = at("low", [P, NT * T], F32, pt_at)
        eqm = at("eqm", [P, NT * T], BF16, pt_at + NT * T * 4)
        gtm = at("gtm", [P, NT * T], BF16, pt_at + NT * T * 6)
        v_at = room(2 * 2 * NT * T * 4)
        v = at("v", [P, 2, 2, NT, QUAD * DH], F32R, v_at)
        yT = at("yT", [P, C, T], F32, v_at)
        z = at("z", [P, NT, D], F32, v_at + 8192)
        x2 = at("x2", [P, NT, D], F32, v_at + 16384)
        tmp = at("tmp", [P, 4, T], F32, v_at + 24576)
        tb = new("tb", [P, T], F32)
        small = new("small", [P, NCOLS], F32)
        ident = new("ident", [P, P], F32)
        ones = new("ones", [P, P], F32)
        halves = new("halves", [P, P], F32)
        before = new("before", [P, P], F32)
        ada = new("ada", [P, 6 * C, B], F32)
        ada1 = new("ada1", [P, 2 * C], F32)
        ada2 = new("ada2", [P, 4 * C], F32)
        scur = new("scur", [P, NT], F32)
        rowmax = new("rowmax", [P, NT], F32)
        nbias = new("nbias", [P, NT], F32)
        rowsum = new("rowsum", [P, NT], F32)
        rinv = new("rinv", [P, NT], F32)
        stats = new("stats", [P, NT, 6], F32)
        meanvar = new("meanvar", [P, NT, 2], F32)
        var = new("var", [P, NT], F32)
        std = new("std", [P, NT], F32)
        rstd = new("rstd", [P, NT], F32)
        newt = new("newt", [P, NT], F32)
        cand = new("cand", [P, 1], F32)
        ncand = new("ncand", [P, 1], F32)
        bit = new("bit", [P, 1], F32)
        nhbit = new("nhbit", [P, 1], F32)
        step_up = new("step_up", [P, 1], F32)
        found = new("found", [P, 1], F32)
        cnt_v = new("cnt_v", [P, 1], F32)
        cnt_s = new("cnt_s", [P, 1], F32)
        n_gt = new("n_gt", [P, 1], F32)
        n_eq = new("n_eq", [P, 1], F32)
        need = new("need", [P, 1], F32)
        rank0 = new("rank0", [P, 1], F32)

        def col(name, i):
            return small[:, COLS[name][0] + i:COLS[name][0] + i + 1]

        bank = [ctx.enter_context(nc.psum_tensor(f"bank{i}", [P, 512], F32)) for i in range(8)]
        total = bank[3]

        def sem(name):
            return ctx.enter_context(nc.semaphore(name))

        small_in, ada_in, xn_in, tb_in = sem("small_in"), sem("ada_in"), sem("xn_in"), sem("tb_in")
        raw_in = [sem("raw_in0"), sem("raw_in1")]
        ident_zero, consts_ready = sem("ident_zero"), sem("consts_ready")
        w_hi, w_ready = sem("w_hi"), sem("w_ready")
        ada_done = sem("ada_done")
        q_done, k_done, v_done, pv_done = sem("q_done"), sem("k_done"), sem("v_done"), sem("pv_done")
        q_hi, k_hi, v_hi, o_hi = sem("q_hi"), sem("k_hi"), sem("v_hi"), sem("o_hi")
        q_lo, k_lo, v_lo, o_lo = sem("q_lo"), sem("k_lo"), sem("v_lo"), sem("o_lo")
        scores, nbias_ready, exp_done, prob_ready = (sem("scores"), sem("nbias_ready"),
                                                     sem("exp_done"), sem("prob_ready"))
        pt_done, pt_hi, pt_lo = sem("pt_done"), sem("pt_hi"), sem("pt_lo")
        y_done, y_gated, y_back = sem("y_done"), sem("y_gated"), sem("y_back")
        var_ready, std_ready, z_ready = sem("var_ready"), sem("std_ready"), sem("z_ready")
        zt_done, xt_hi, xt_lo = sem("zt_done"), sem("xt_hi"), sem("xt_lo")
        f_done, g_done, h_hi, h_lo = sem("f_done"), sem("g_done"), sem("h_hi"), sem("h_lo")
        y2_done, y2_gated, y2_back, out_ready = (sem("y2_done"), sem("y2_gated"), sem("y2_back"),
                                                 sem("out_ready"))
        xmax_ready, xexp_done, adj_ready, diag_done = (sem("xmax_ready"), sem("xexp_done"),
                                                       sem("adj_ready"), sem("diag_done"))
        cand_ready, counted_v, counted_s, total_ready = (sem("cand_ready"), sem("counted_v"),
                                                         sem("counted_s"), sem("total_ready"))
        ties_counted, ranks_ready, xm_ready = sem("ties_counted"), sem("ranks_ready"), sem("xm_ready")
        out_stored = sem("out_stored")
        waits_met = sem("waits_met")

        W_CREDIT = 2
        Y2_CREDIT = C

        block = ctx.enter_context(nc.Block())

        x_seq = x.rearrange("b (p i) d -> b p (i d)", p=P)
        out_seq = out.rearrange("b (p i) d -> b p (i d)", p=P)

        def seq(view, b):
            return view[b] if isinstance(b, int) else view[bass.ds(b, 1)].rearrange("a p n -> (a p) n")

        def wait_apart(eng, signal, value):
            eng.wait_ge(signal, value)
            eng.sem_inc(waits_met, 1)

        def w_wait(eng, b, n):
            eng.wait_ge(w_ready, b * NHALF + (n + 1 + W_CREDIT))

        @block.sync
        def _(sp):
            pairs = weights.rearrange("(m s) p n -> m s p n", s=2)

            def load_halves(b, lo, hi):
                with sp.Fori(lo // 2, hi // 2) as m:
                    for slot in range(2):
                        wait_apart(sp, w_ready, b * NHALF + m * 2 + (slot + W_CREDIT - 1))
                        src = pairs[bass.ds(m, 1), slot].rearrange("a p n -> (a p) n")
                        sp.dma_start(wraw[:, slot, :], src).then_inc(raw_in[slot], 16)

            def load_x(b):
                sp.dma_start(xn[:, :, :].rearrange("p i d -> p (i d)"), seq(x_seq, b)).then_inc(xn_in, 16)
                row = cond[b:b + 1, :] if isinstance(b, int) else cond[bass.ds(b, 1), :]
                sp.dma_start(tb[:, :], row.to_broadcast([P, T])).then_inc(tb_in, 16)

            def store(b):
                wait_apart(sp, out_ready, b + 1)
                sp.dma_start(seq(out_seq, b), xn[:, :, :].rearrange("p i d -> p (i d)"))\
                    .then_inc(out_stored, 16)

            def sequence(b, first=False, last=False):
                load_halves(b, 0, 8)
                if not first:
                    store(b - 1)
                    wait_apart(sp, out_stored, b * 16)
                if not last:
                    wait_apart(sp, xm_ready, b + 1)
                    load_x(b + 1)
                load_halves(b, 8, NHALF)

            load_x(0)
            sp.dma_start(small[:, :], cols).then_inc(small_in, 16)
            for c in range(C):
                sp.dma_start(adaw[:, c, :], ada_w[c * P:(c + 1) * P, :]).then_inc(ada_in, 16)
            sequence(0, first=True)
            with sp.Fori(1, B - 1) as b:
                sequence(b)
            sequence(B - 1, last=True)
            store(B - 1)
            sp.wait_ge(out_stored, 16 * B)

        @block.gpsimd
        def _(pool):
            minus_inf = pool.to_reg(float("-inf"))
            nc.gpsimd.memset(ident[:, :], 0.0).then_inc(ident_zero, 1)
            nc.gpsimd.memset(ones[:, :], 1.0).then_inc(ident_zero, 1)
            nc.gpsimd.memset(halves[:, :], 0.5).then_inc(consts_ready, 1)
            pool.wait_ge(ident_zero, 2)
            nc.gpsimd.affine_select(out=ident[:, :], in_=ident[:, :], compare_op=ALU.not_equal, fill=1.0,
                                    base=0, pattern=[[-1, P]], channel_multiplier=1).then_inc(consts_ready, 1)
            nc.gpsimd.affine_select(out=before[:, :], in_=ones[:, :], compare_op=ALU.is_gt, fill=0.0,
                                    base=0, pattern=[[1, P]], channel_multiplier=-1).then_inc(consts_ready, 1)
            pool.sem_inc(w_ready, W_CREDIT)

            def clear_diagonal(t):
                wait_apart(pool, adj_ready, t + 1)
                nc.gpsimd.affine_select(out=prob[:, :, :], in_=prob[:, :, :], compare_op=ALU.not_equal,
                                        fill=minus_inf, base=0, pattern=[[-1, NT], [1, T]],
                                        channel_multiplier=-NT).then_inc(diag_done, 1)

            def split(b, n, region, half):
                wait_apart(pool, raw_in[n % 2], b * (16 * NHALF // 2) + 16 * (n // 2 + 1))
                span = slice(half * HALF, (half + 1) * HALF)
                nc.gpsimd.tensor_copy(w[:, region, 0, span], wraw[:, n % 2, :]).then_inc(w_hi, 1)
                pool.wait_ge(w_hi, b * NHALF + (n + 1))
                nc.gpsimd.tensor_tensor(w[:, region, 1, span], wraw[:, n % 2, :],
                                        w[:, region, 0, span].bitcast(F32), ALU.subtract)\
                    .then_inc(w_ready, 1)

            def split_v(b, q):
                if q:
                    pool.wait_ge(v_done, b * H + QUAD * q)
                else:
                    pool.wait_ge(y2_done, b * C + (Y2_CREDIT - 1))
                split(b, v_half(q, 0), 0, 0)
                split(b, v_half(q, 1), 0, 1)

            def split_qk(b, h):
                if h >= 2:
                    pool.wait_ge(k_done, b * H + (h - 1))
                elif h == 0:
                    pool.wait_ge(y2_done, b * C + Y2_CREDIT)
                split(b, qk_half(h), 1, h % 2)

            def sequence(b, last=False):
                split_v(b, 0)
                split_qk(b, 0)
                split_qk(b, 1)
                for q in range(3):
                    split_v(b, q + 1)
                    for h in range(4 * q + 2, 4 * q + 6):
                        split_qk(b, h)
                split_qk(b, 14)
                split_qk(b, 15)
                for u in range(NUNIT):
                    if u == 0:
                        pool.wait_ge(v_done, b * H + H)
                    elif u == 1:
                        pool.wait_ge(k_done, b * H + H)
                    elif u < 6:
                        pool.wait_ge(y_done, b * C + (u - 1))
                    elif u < 10:
                        pool.wait_ge(f_done, b * KC + 4 * (u - 5))
                    else:
                        pool.wait_ge(y2_done, b * C + (Y2_CREDIT + u - 9))
                    for half in range(2):
                        split(b, NQKV + 2 * u + half, u % 2, half)
                    if u == 1 and not last:
                        clear_diagonal(b + 1)

            clear_diagonal(0)
            with pool.Fori(0, B - 1) as b:
                sequence(b)
            sequence(B - 1, last=True)

        @block.scalar
        def _(act_e):
            def topk_exp(t):
                act_e.wait_ge(xmax_ready, t + 1)
                for i in range(NT):
                    ins = nc.scalar.activation(prob[:, i, :], xn[:, i, :], ACT.Exp, bias=nbias[:, i:i + 1],
                                               accum_out=rowsum[:, i:i + 1])
                ins.then_inc(xexp_done, 1)

            def topk_count(t, step):
                src = keys16[:, NCOUNT:, 1] if step < LEVEL else low[:, NCOUNT:]
                act_e.wait_ge(cand_ready, t * STEPS + (step + 1))
                nc.scalar.activation(gtm[:, 0:NCOUNT], src, ACT.Sign, bias=ncand[:, :],
                                     accum_out=cnt_s[:, :]).then_inc(counted_s, 1)

            def ln(k, shift, scale1):
                act_e.wait_ge(var_ready, k + 1)
                nc.scalar.activation(std[:, :], var[:, :], ACT.Sqrt).then_inc(std_ready, 1)
                for c in range(C):
                    act_e.wait_ge(zt_done, k * C + (c + 1))
                    nc.scalar.activation(xT[:, 0, c, :], bank[c][:, :], ACT.Identity,
                                         bias=shift[:, c:c + 1], scale=scale1[:, c:c + 1]).then_inc(xt_hi, 1)

            def v_part(b, idx):
                act_e.wait_ge(v_done, b * H + (idx + 1))
                bk = bank[4 + idx] if idx < 4 else bank[7]
                nc.scalar.copy(v[:, (idx // 4) % 2, 0, idx % 4, :], bk[:, :]).then_inc(v_hi, 1)

            def qk_part(b, h):
                act_e.wait_ge(q_done, b * H + (h + 1))
                nc.scalar.activation(qk[:, 0, 0, :], bank[4][:, :], ACT.Identity, bias=col("bq", h))\
                    .then_inc(q_hi, 1)
                act_e.wait_ge(k_done, b * H + (h + 1))
                nc.scalar.activation(qk[:, 1, 0, :], bank[5][:, :], ACT.Identity, bias=col("bk", h))\
                    .then_inc(k_hi, 1)

            def head(b, h):
                for i in range(NT):
                    act_e.wait_ge(nbias_ready, b * (H * NT) + (h * NT + i + 1))
                    nc.scalar.activation(prob[:, i, :], bank[i][:, :], ACT.Exp, bias=nbias[:, i:i + 1],
                                         scale=SCALE, accum_out=rowsum[:, i:i + 1]).then_inc(exp_done, 1)
                if h + 1 < H:
                    qk_part(b, h + 1)
                for j in range(NT):
                    act_e.wait_ge(pt_done, b * (H * NT) + (h * NT + j + 1))
                    nc.scalar.copy(probT[:, 0, j, :], bank[j][:, :]).then_inc(pt_hi, 1)
                if h + QUAD < H:
                    v_part(b, h + QUAD)
                act_e.wait_ge(pv_done, b * H + (h + 1))
                nc.scalar.activation(act[:, 0, h, :], bank[6][:, :], ACT.Identity, bias=col("bv", h))\
                    .then_inc(o_hi, 1)

            def sequence(b, last=False):
                for idx in range(QUAD):
                    v_part(b, idx)
                qk_part(b, 0)
                for h in range(H):
                    head(b, h)
                if not last:
                    topk_exp(b + 1)
                    topk_count(b + 1, 0)
                for u in range(4):
                    for r in range(4):
                        slot = SLOTS.get(("out", u, r))
                        if not last and slot is not None and slot + 1 < STEPS:
                            topk_count(b + 1, slot + 1)
                ln(b * 2 + 1, ada2[:, C:2 * C], ada2[:, 2 * C:3 * C])
                for f in range(KC):
                    slot = SLOTS.get(("mlp_in", f // 4, f % 4))
                    if not last and slot is not None and slot + 1 < STEPS:
                        topk_count(b + 1, slot + 1)
                    act_e.wait_ge(f_done, b * KC + (f + 1))
                    if f >= 4:
                        act_e.wait_ge(h_lo, b * KC + (f - 3))
                    nc.scalar.activation(tmp[:, f % 4, :], bank[4 + f % 4][:, :], ACT.Gelu,
                                         bias=col("b1", f)).then_inc(g_done, 1)
                    nc.scalar.activation(act[:, 0, f, :], bank[4 + f % 4][:, :], ACT.Gelu,
                                         bias=col("b1", f)).then_inc(h_hi, 1)
                if not last:
                    for u in range(4):
                        for r in range(4):
                            slot = SLOTS.get(("mlp_out", u, r))
                            if slot is not None and slot + 1 < STEPS:
                                topk_count(b + 1, slot + 1)
                    ln(b * 2 + 2, ada1[:, 0:C], ada1[:, C:2 * C])

            act_e.wait_ge(small_in, 16)
            topk_exp(0)
            for step in range(STEPS):
                topk_count(0, step)
            ln(0, ada1[:, 0:C], ada1[:, C:2 * C])
            with act_e.Fori(0, B - 1) as b:
                sequence(b)
            sequence(B - 1, last=True)

        @block.vector
        def _(dve):
            V = nc.vector

            def count(t, step):
                src = keys16[:, :NCOUNT, 1] if step < LEVEL else low[:, :NCOUNT]
                V.tensor_scalar(eqm[:, 0:NCOUNT], src, cand[:, :], None, op0=ALU.is_ge, op1=ALU.add,
                                accum_out=cnt_v[:, :]).then_inc(counted_v, 1)

            def start_level(t, step):
                V.memset(cand[:, :], TOP_BIT)
                V.memset(bit[:, :], TOP_BIT)
                V.memset(nhbit[:, :], -TOP_BIT / 2)
                V.memset(ncand[:, :], 0.5 - TOP_BIT).then_inc(cand_ready, 1)
                dve.drain()
                count(t, step)

            def topk_keys(t):
                dve.wait_ge(xn_in, t * 16 + 16)
                V.tensor_reduce(nbias[:, :], xn[:, :, :], AX.X, ALU.max, negate=True).then_inc(xmax_ready, 1)
                src = small[:, COLS["s"][0]:COLS["s"][1]].rearrange("p (b i) -> p b i", b=B)
                V.tensor_copy(scur[:, :], src[:, t, :] if isinstance(t, int) else
                              src[:, bass.ds(t, 1), :].rearrange("p a i -> p (a i)"))
                dve.wait_ge(xexp_done, t + 1)
                V.reciprocal(rinv[:, :], rowsum[:, :])
                dve.drain()
                for i in range(NT):
                    V.tensor_scalar(prob[:, i, :], prob[:, i, :], rinv[:, i:i + 1], float(np.float32(T ** -0.5)),
                                    ALU.mult, ALU.mult)
                dve.drain()
                dve.wait_ge(tb_in, t * 16 + 16)
                for i in range(NT):
                    ins = V.scalar_tensor_tensor(prob[:, i, :], tb[:, :], scur[:, i:i + 1], prob[:, i, :],
                                                 ALU.mult, ALU.mult)
                ins.then_inc(adj_ready, 1)
                dve.wait_ge(diag_done, t + 1)
                V.tensor_scalar(flip[:, :], keys, 31, -(1 << 31), ALU.arith_shift_right, ALU.bitwise_or)
                dve.drain()
                V.tensor_tensor(keys, keys, flip[:, :], ALU.bitwise_xor)
                dve.drain()
                start_level(t, 0)

            def topk_step(t, step):
                dve.wait_ge(total_ready, t * STEPS + (step + 1))
                V.tensor_scalar(step_up[:, :], total[:, 0:1], float(KTOP - P * NCOUNT // 2) - 0.5, bit[:, :],
                                ALU.is_gt, ALU.mult)
                dve.drain()
                V.scalar_tensor_tensor(cand[:, :], step_up[:, :], nhbit[:, :], cand[:, :], ALU.add, ALU.add)
                dve.drain()
                if step % LEVEL != LEVEL - 1:
                    V.tensor_scalar(ncand[:, :], cand[:, :], -1.0, 0.5, ALU.mult, ALU.add).then_inc(cand_ready, 1)
                    V.tensor_scalar(bit[:, :], bit[:, :], 0.5, None, ALU.mult)
                    V.tensor_scalar(nhbit[:, :], nhbit[:, :], 0.5, None, ALU.mult)
                    count(t, step + 1)
                    return
                V.tensor_scalar(found[:, :], cand[:, :], -0.5, None, ALU.add)
                dve.drain()
                if step < LEVEL:
                    V.tensor_scalar(low[:, :], keys16[:, :, 1], found[:, :], float(1 << 17),
                                    ALU.subtract, ALU.mult)
                    dve.drain()
                    V.tensor_tensor(low[:, :], low[:, :], keys16[:, :, 0], ALU.add)
                    dve.drain()
                    start_level(t, step + 1)
                else:
                    V.tensor_scalar(eqm[:, :], low[:, :], found[:, :], None, op0=ALU.is_equal, op1=ALU.add,
                                    accum_out=n_eq[:, :])
                    V.tensor_scalar(gtm[:, :], low[:, :], found[:, :], None, op0=ALU.is_gt, op1=ALU.add,
                                    accum_out=n_gt[:, :]).then_inc(ties_counted, 1)

            def topk_mask(t):
                dve.wait_ge(ranks_ready, t + 1)
                V.tensor_scalar(need[:, :], total[:, 0:1], -1.0, float(KTOP), ALU.mult, ALU.add)
                V.tensor_copy(rank0[:, :], total[:, 1:2])
                dve.drain()
                V.tensor_tensor_scan(rank, eqm[:, :], eqm[:, :], rank0[:, :], ALU.add, ALU.max)
                dve.drain()
                V.scalar_tensor_tensor(eqm[:, :], rank, need[:, :], eqm[:, :], ALU.is_le, ALU.mult)
                dve.drain()
                V.tensor_tensor(gtm[:, :], gtm[:, :], eqm[:, :], ALU.add)
                dve.drain()
                V.tensor_tensor(xm[:, :, :].rearrange("p i d -> p (i d)"),
                                xn[:, :, :].rearrange("p i d -> p (i d)"), gtm[:, :], ALU.add)\
                    .then_inc(xm_ready, 1)
                dve.drain()

            def normalise(k, src):
                for i in range(NT):
                    V.bn_stats(stats[:, i, :], src[:, i, :])
                dve.drain()
                for i in range(NT):
                    V.bn_aggr(meanvar[:, i, :], stats[:, i, :])
                dve.drain()
                V.tensor_scalar(var[:, :], meanvar[:, :, 1], EPS, None, ALU.add).then_inc(var_ready, 1)
                dve.wait_ge(std_ready, k + 1)
                V.reciprocal(rstd[:, :], std[:, :])
                dve.drain()
                V.tensor_tensor(newt[:, :], rstd[:, :], rstd[:, :], ALU.mult)
                dve.drain()
                V.tensor_tensor(newt[:, :], newt[:, :], var[:, :], ALU.mult)
                dve.drain()
                V.tensor_scalar(newt[:, :], newt[:, :], -0.5, 1.5, ALU.mult, ALU.add)
                dve.drain()
                V.tensor_tensor(rstd[:, :], rstd[:, :], newt[:, :], ALU.mult)
                dve.drain()
                for i in range(NT):
                    V.tensor_scalar(z[:, i, :], src[:, i, :], meanvar[:, i, 0:1], rstd[:, i:i + 1],
                                    ALU.subtract, ALU.mult).then_inc(z_ready, 1)

            def modulate(k, shift, scale1):
                for c in range(C):
                    dve.wait_ge(xt_hi, k * C + (c + 1))
                    V.tensor_scalar(tmp[:, c, :], bank[c][:, :], scale1[:, c:c + 1], shift[:, c:c + 1],
                                    ALU.mult, ALU.add)
                    dve.drain()
                    V.tensor_tensor(xT[:, 1, c, :], tmp[:, c, :], xT[:, 0, c, :].bitcast(F32), ALU.subtract)\
                        .then_inc(xt_lo, 1)

            def v_part(b, idx):
                dve.wait_ge(v_hi, b * H + (idx + 1))
                bk = bank[4 + idx] if idx < 4 else bank[7]
                V.tensor_tensor(v[:, (idx // 4) % 2, 1, idx % 4, :], bk[:, :],
                                v[:, (idx // 4) % 2, 0, idx % 4, :].bitcast(F32), ALU.subtract).then_inc(v_lo, 1)

            def biased_lo(dst, src, bias, hi):
                return V.scalar_tensor_tensor(dst, src, bias, hi.bitcast(F32), ALU.add, ALU.subtract)

            def qk_part(b, h):
                dve.wait_ge(q_hi, b * H + (h + 1))
                biased_lo(qk[:, 0, 1, :], bank[4][:, :], col("bq", h), qk[:, 0, 0, :]).then_inc(q_lo, 1)
                dve.wait_ge(k_hi, b * H + (h + 1))
                biased_lo(qk[:, 1, 1, :], bank[5][:, :], col("bk", h), qk[:, 1, 0, :]).then_inc(k_lo, 1)

            def head(b, h):
                tile = h * NT
                for i in range(NT + 1):
                    if i < NT:
                        dve.wait_ge(scores, b * (H * NT) + (tile + i + 1))
                        V.reduce_max(rowmax[:, i:i + 1], bank[i][:, :], AX.X)
                    if i:
                        dve.wait_ge(exp_done, b * (H * NT) + (tile + i))
                        V.reciprocal(rinv[:, i - 1:i], rowsum[:, i - 1:i])
                    dve.drain()
                    if i < NT:
                        V.tensor_scalar(nbias[:, i:i + 1], rowmax[:, i:i + 1], -SCALE, None, ALU.mult)\
                            .then_inc(nbias_ready, 1)
                    if i:
                        V.tensor_scalar(prob[:, i - 1, :], prob[:, i - 1, :], rinv[:, i - 1:i], None, ALU.mult)\
                            .then_inc(prob_ready, 1)
                if h + 1 < H:
                    qk_part(b, h + 1)
                for j in range(NT):
                    dve.wait_ge(pt_hi, b * (H * NT) + (tile + j + 1))
                    V.tensor_tensor(probT[:, 1, j, :], bank[j][:, :], probT[:, 0, j, :].bitcast(F32),
                                    ALU.subtract).then_inc(pt_lo, 1)
                if h + QUAD < H:
                    v_part(b, h + QUAD)
                dve.wait_ge(o_hi, b * H + (h + 1))
                biased_lo(act[:, 1, h, :], bank[6][:, :], col("bv", h), act[:, 0, h, :]).then_inc(o_lo, 1)

            def gate(done, gated, b, u, bias, gates):
                dve.wait_ge(done, b * C + (u + 1 + (Y2_CREDIT if done is y2_done else 0)))
                V.tensor_scalar(yT[:, u, :], bank[4 + u][:, :], col(bias, u), gates[:, u:u + 1],
                                ALU.add, ALU.mult).then_inc(gated, 1)

            def hidden_lo(b, f):
                dve.wait_ge(h_hi, b * KC + (f + 1))
                V.tensor_tensor(act[:, 1, f, :], tmp[:, f % 4, :], act[:, 0, f, :].bitcast(F32),
                                ALU.subtract).then_inc(h_lo, 1)

            def sequence(b, last=False):
                src = ada[:, 2 * C:6 * C, b] if isinstance(b, int) else \
                    ada[:, 2 * C:6 * C, bass.ds(b, 1)].rearrange("p c a -> p (c a)")
                V.tensor_copy(ada2[:, :], src)
                for idx in range(QUAD):
                    v_part(b, idx)
                qk_part(b, 0)
                for h in range(H):
                    head(b, h)
                if not last:
                    topk_keys(b + 1)
                for u in range(4):
                    for r in range(4):
                        step = SLOTS.get(("out", u, r))
                        if not last and step is not None:
                            topk_step(b + 1, step)
                        if r == 0 and u:
                            gate(y_done, y_gated, b, u - 1, "ob", ada2[:, 0:C])
                gate(y_done, y_gated, b, 3, "ob", ada2[:, 0:C])
                for i in range(NT):
                    dve.wait_ge(y_back, b * NT + (i + 1))
                    V.tensor_tensor(x2[:, i, :], xm[:, i, :], bank[i][:, :], ALU.add)
                dve.drain()
                normalise(b * 2 + 1, x2)
                modulate(b * 2 + 1, ada2[:, C:2 * C], ada2[:, 2 * C:3 * C])
                V.tensor_tensor(x2[:, :, :].rearrange("p i d -> p (i d)"),
                                x2[:, :, :].rearrange("p i d -> p (i d)"),
                                xm[:, :, :].rearrange("p i d -> p (i d)"), ALU.add)
                for f in range(KC):
                    step = SLOTS.get(("mlp_in", f // 4, f % 4))
                    if not last and step is not None:
                        topk_step(b + 1, step)
                    if f:
                        hidden_lo(b, f - 1)
                hidden_lo(b, KC - 1)
                if not last:
                    for u in range(4):
                        for r in range(4):
                            step = SLOTS.get(("mlp_out", u, r))
                            if step is not None:
                                topk_step(b + 1, step)
                    gate(y2_done, y2_gated, b, 0, "b2", ada2[:, 3 * C:4 * C])
                    topk_mask(b + 1)
                    next_modulation(b + 1)
                    normalise(b * 2 + 2, xm)
                    gate(y2_done, y2_gated, b, 1, "b2", ada2[:, 3 * C:4 * C])
                    gate(y2_done, y2_gated, b, 2, "b2", ada2[:, 3 * C:4 * C])
                    modulate(b * 2 + 2, ada1[:, 0:C], ada1[:, C:2 * C])
                else:
                    for u in range(3):
                        gate(y2_done, y2_gated, b, u, "b2", ada2[:, 3 * C:4 * C])
                gate(y2_done, y2_gated, b, 3, "b2", ada2[:, 3 * C:4 * C])
                for i in range(NT):
                    dve.wait_ge(y2_back, b * NT + (i + 1))
                    ins = V.tensor_tensor(xn[:, i, :], x2[:, i, :], bank[i][:, :], ALU.add)
                ins.then_inc(out_ready, 1)

            def next_modulation(t):
                src = ada[:, 0:2 * C, t] if isinstance(t, int) else \
                    ada[:, 0:2 * C, bass.ds(t, 1)].rearrange("p c a -> p (c a)")
                V.tensor_copy(ada1[:, :], src)

            dve.wait_ge(small_in, 16)
            topk_keys(0)
            for step in range(STEPS):
                topk_step(0, step)
            dve.wait_ge(ada_done, 1)
            ada_b = small[:, COLS["ada_b"][0]:COLS["ada_b"][1]]
            V.tensor_tensor(ada[:, :, :], bank[0][:, 0:6 * C * B].rearrange("p (m b) -> p m b", b=B),
                            ada_b.unsqueeze(2).to_broadcast([P, 6 * C, B]), ALU.add)
            dve.drain()
            for part in (1, 4):
                V.tensor_scalar(ada[:, part * C:(part + 1) * C, :], ada[:, part * C:(part + 1) * C, :],
                                1.0, None, ALU.add)
            dve.drain()
            next_modulation(0)
            topk_mask(0)
            normalise(0, xm)
            modulate(0, ada1[:, 0:C], ada1[:, C:2 * C])
            V.memset(newt[:, :], 0.0).then_inc(o_lo, 1)
            with dve.Fori(0, B - 1) as b:
                sequence(b)
            sequence(B - 1, last=True)

        @block.tensor
        def _(pe):
            def mm3(dst, w_hi_ap, w_lo_ap, x_hi_ap, x_lo_ap, first, last):
                pe.matmul(dst, w_hi_ap, x_hi_ap, start=first, stop=False)
                pe.matmul(dst, w_hi_ap, x_lo_ap, start=False, stop=False)
                return pe.matmul(dst, w_lo_ap, x_hi_ap, start=False, stop=last)

            def take_total(t, step):
                pe.wait_ge(counted_v, t * STEPS + (step + 1))
                pe.wait_ge(counted_s, t * STEPS + (step + 1))
                pe.matmul(total[:, 0:1], ones[:, :], cnt_v[:, :], start=True, stop=False)
                pe.matmul(total[:, 0:1], halves[:, :], cnt_s[:, :], start=False, stop=True)\
                    .then_inc(total_ready, 1)

            def take_ranks(t):
                pe.wait_ge(ties_counted, t + 1)
                pe.matmul(total[:, 0:1], ones[:, :], n_gt[:, :], start=True, stop=True)
                pe.matmul(total[:, 1:2], before[:, :], n_eq[:, :], start=True, stop=True)\
                    .then_inc(ranks_ready, 1)

            def transpose_z(k):
                pe.wait_ge(z_ready, k * NT + NT)
                for c in range(C):
                    for i in range(NT):
                        ins = pe.transpose(bank[c][:, i * P:(i + 1) * P], z[:, i, c * P:(c + 1) * P], ident[:, :])
                    ins.then_inc(zt_done, 1)

            def v_tile(b, idx):
                q, m = idx // 4, idx % 4
                bk = bank[4 + idx] if q == 0 else bank[7]
                if m == 0:
                    w_wait(pe, b, v_half(q, 1))
                if q:
                    pe.wait_ge(v_lo, b * H + idx)
                for c in range(C):
                    part = slice(c * T, (c + 1) * T)
                    rows = slice(m * P, (m + 1) * P)
                    ins = mm3(bk[:, :], xT[:, 0, c, rows], xT[:, 1, c, rows], w[:, 0, 0, part], w[:, 0, 1, part],
                              c == 0, c == C - 1)
                ins.then_inc(v_done, 1)

            def qk_proj(b, h):
                w_wait(pe, b, qk_half(h))
                for which, bk, done in ((0, bank[4], q_done), (1, bank[5], k_done)):
                    if h == 0:
                        pe.wait_ge(v_lo, b * H + (which + 1))
                    for c in range(C):
                        part = slice((h % 2) * HALF + c * 2 * P + which * P, (h % 2) * HALF + c * 2 * P + which * P + P)
                        ins = mm3(bk[:, :], w[:, 1, 0, part], w[:, 1, 1, part], xT[:, 0, c, :], xT[:, 1, c, :],
                                  c == 0, c == C - 1)
                    ins.then_inc(done, 1)

            def head(b, h):
                pe.wait_ge(q_lo, b * H + (h + 1))
                pe.wait_ge(k_lo, b * H + (h + 1))
                for i in range(NT):
                    rows = slice(i * P, (i + 1) * P)
                    mm3(bank[i][:, :], qk[:, 0, 0, rows], qk[:, 0, 1, rows], qk[:, 1, 0, :], qk[:, 1, 1, :],
                        True, True).then_inc(scores, 1)
                if h + 1 < H:
                    qk_proj(b, h + 1)
                pe.wait_ge(prob_ready, b * (H * NT) + (h * NT + NT))
                for j in range(NT):
                    for i in range(NT):
                        ins = pe.transpose(bank[j][:, i * P:(i + 1) * P], prob[:, i, j * P:(j + 1) * P], ident[:, :])
                    ins.then_inc(pt_done, 1)
                if h + QUAD < H:
                    v_tile(b, h + QUAD)
                q, m = h // QUAD, h % QUAD
                if m == 0:
                    pe.wait_ge(v_lo, b * H + 4 * (q + 1))
                pe.wait_ge(o_lo, b * H + (h + 1))
                for j in range(NT):
                    pe.wait_ge(pt_lo, b * (H * NT) + (h * NT + j + 1))
                    part = slice(m * P, (m + 1) * P)
                    ins = mm3(bank[6][:, :], v[:, q % 2, 0, j, part], v[:, q % 2, 1, j, part],
                              probT[:, 0, j, :], probT[:, 1, j, :], j == 0, j == NT - 1)
                ins.then_inc(pv_done, 1)

            def transpose_back(src, b, gated, back):
                pe.wait_ge(gated, b * C + C)
                for i in range(NT):
                    for u in range(C):
                        ins = pe.transpose(bank[i][:, u * P:(u + 1) * P], src[:, u, i * P:(i + 1) * P], ident[:, :])
                    ins.then_inc(back, 1)

            def wide_unit(b, phase, u, last, done):
                unit = (0 if phase == "out" else 8) + u
                for kc in range(KC):
                    if kc % 8 == 0:
                        w_wait(pe, b, NQKV + 2 * unit + kc // 8)
                    if phase == "out" and u == 0 and kc == KC - 1:
                        pe.wait_ge(o_lo, b * H + (H + 1))
                    if phase == "mlp_out" and kc == 0:
                        pe.wait_ge(h_hi, b * KC + (KC - 3 + u))
                    if phase == "mlp_out" and u == 0 and (kc % 4 == 0 or kc == KC - 1):
                        pe.wait_ge(h_lo, b * KC + (KC if kc == KC - 1 else min(kc + 4, KC - 1)))
                    part = slice(kc * P, (kc + 1) * P)
                    ins = mm3(bank[4 + u][:, :], w[:, unit % 2, 0, part], w[:, unit % 2, 1, part],
                              act[:, 0, kc, :], act[:, 1, kc, :], kc == 0, kc == KC - 1)
                    if kc == KC - 1:
                        ins.then_inc(done, 1)
                    if kc % 4 == 3 and not last:
                        between(b, (phase, u, kc // 4))

            def between(b, place):
                if place in SLOTS:
                    take_total(b + 1, SLOTS[place])
                if place == RANK_SLOT:
                    take_ranks(b + 1)
                if place == LN1_SLOT:
                    transpose_z(b * 2 + 2)

            def mlp_in(b, last):
                for f in range(KC):
                    unit = 4 + f // 4
                    if f % 4 == 0:
                        w_wait(pe, b, NQKV + 2 * unit + 1)
                    if f >= 4:
                        pe.wait_ge(h_hi, b * KC + (f - 3))
                    for c in range(C):
                        part = slice(c * T + (f % 4) * P, c * T + (f % 4 + 1) * P)
                        ins = mm3(bank[4 + f % 4][:, :], w[:, unit % 2, 0, part], w[:, unit % 2, 1, part],
                                  xT[:, 0, c, :], xT[:, 1, c, :], c == 0, c == C - 1)
                    ins.then_inc(f_done, 1)
                    if not last:
                        between(b, ("mlp_in", f // 4, f % 4))

            def sequence(b, last=False):
                pe.wait_ge(xt_lo, b * (2 * C) + C)
                for idx in range(QUAD):
                    v_tile(b, idx)
                qk_proj(b, 0)
                for h in range(H):
                    head(b, h)
                for u in range(4):
                    wide_unit(b, "out", u, last, y_done)
                transpose_back(yT, b, y_gated, y_back)
                transpose_z(b * 2 + 1)
                pe.wait_ge(xt_lo, b * (2 * C) + 2 * C)
                mlp_in(b, last)
                for u in range(4):
                    wide_unit(b, "mlp_out", u, last, y2_done)
                if not last:
                    pe.wait_ge(xt_lo, b * (2 * C) + 3 * C)
                transpose_back(yT, b, y2_gated, y2_back)

            pe.sem_inc(y2_done, Y2_CREDIT)
            pe.wait_ge(consts_ready, 3)
            for step in range(LEVEL):
                take_total(0, step)
            pe.wait_ge(small_in, 16)
            pe.wait_ge(ada_in, 16 * C)
            c0 = COLS["cond"][0]
            for m in range(6 * C):
                for c in range(C):
                    ins = pe.matmul(bank[0][:, m * B:(m + 1) * B], adaw[:, c, m * P:(m + 1) * P],
                                    small[:, c0 + c * B:c0 + (c + 1) * B], start=c == 0, stop=c == C - 1)
            ins.then_inc(ada_done, 1)
            for step in range(LEVEL, STEPS):
                take_total(0, step)
            take_ranks(0)
            transpose_z(0)
            with pe.Fori(0, B - 1) as b:
                sequence(b)
            sequence(B - 1, last=True)


def _half_units(qkv_w, out_w, w1, w2):
    n = H * DH
    q = qkv_w.reshape(C, P, 3 * n)

    def pack(a):
        return a.transpose(1, 0, 2).reshape(P, -1)

    halves = np.empty((NHALF, P, HALF), qkv_w.dtype)
    for h in range(H):
        one = np.concatenate([q[:, :, h * DH:(h + 1) * DH], q[:, :, n + h * DH:n + (h + 1) * DH]], axis=2)
        halves[qk_half(h)] = pack(one)
    for g in range(H // QUAD):
        one = pack(q[:, :, 2 * n + g * QUAD * DH:2 * n + (g + 1) * QUAD * DH])
        halves[v_half(g, 0)], halves[v_half(g, 1)] = one[:, :HALF], one[:, HALF:]
    for u in range(4):
        units = (pack(out_w.reshape(KC, P, D)[:, :, u * P:(u + 1) * P]),
                 pack(w1.reshape(C, P, F)[:, :, u * T:(u + 1) * T]),
                 pack(w2.reshape(KC, P, D)[:, :, u * P:(u + 1) * P]))
        for layer, one in enumerate(units):
            at = NQKV + 8 * layer + 2 * u
            halves[at], halves[at + 1] = one[:, :HALF], one[:, HALF:]
    return halves


def kernel(x, fside_BxSx1_0, cond_2048, L1_cond_ada_w, L1_cond_ada_b, L1_cond_qkv_w, L1_cond_qkv_b,
           L1_cond_out_w, L1_cond_out_b, L1_cond_ffn_w1, L1_cond_ffn_b1, L1_cond_ffn_w2, L1_cond_ffn_b2):
    import concourse.bacc as bacc
    from concourse.bass_utils import run_bass_kernel_spmd

    x, s, cond, ada_w, ada_b, qkv_w, qkv_b, out_w, out_b, w1, b1, w2, b2 = (
        np.asarray(a) for a in (x, fside_BxSx1_0, cond_2048, L1_cond_ada_w, L1_cond_ada_b, L1_cond_qkv_w,
                                L1_cond_qkv_b, L1_cond_out_w, L1_cond_out_b, L1_cond_ffn_w1, L1_cond_ffn_b1,
                                L1_cond_ffn_w2, L1_cond_ffn_b2))

    def columns(a):
        return a.reshape(-1, P).T

    cols = np.concatenate([
        columns(qkv_b), columns(out_b), columns(b1), columns(b2), columns(ada_b),
        s.reshape(B, P, NT).transpose(1, 0, 2).reshape(P, B * NT),
        cond.reshape(B, C, P).transpose(2, 1, 0).reshape(P, C * B)], axis=1)
    arrays = {"x_in": np.ascontiguousarray(x), "cond_in": np.ascontiguousarray(cond),
              "weights_in": _half_units(qkv_w, out_w, w1, w2), "ada_w_in": np.ascontiguousarray(ada_w),
              "cols_in": np.ascontiguousarray(cols)}
    nc = bacc.Bacc("TRN2", target_bir_lowering=False, num_devices=1)
    args = [nc.dram_tensor(name, a.shape, mybir.dt.from_np(a.dtype), kind="ExternalInput").ap()
            for name, a in arrays.items()]
    out = nc.dram_tensor("out", (B, T, D), F32, kind="ExternalOutput").ap()
    block_kernel(nc, *args, out)
    return run_bass_kernel_spmd(nc, [arrays], core_ids=[0]).results[0]["out"]
```

```python
from contextlib import ExitStack

import numpy as np

import concourse.bass as bass
from concourse import mybir

F32 = mybir.dt.float32
F32R = mybir.dt.float32r
I32 = mybir.dt.int32
U16 = mybir.dt.uint16
BF16 = mybir.dt.bfloat16
F16 = mybir.dt.float16
ALU = mybir.AluOpType
ACT = mybir.ActivationFunctionType
AX = mybir.AxisListType

P = 128
B, T, D = 4, 512, 512
H, DH = 16, 128
F = 2048
KTOP = 5120
EPS = 1e-6
SCALE = DH ** -0.5
C = D // P
NT = T // P
KC = F // P
HALF = 1024
QUAD = 4
NHALF = 48
NQKV = 24
NUNIT = 12
STEPS = 32
LEVEL = 16
NCOUNT = T * T // P // 2
EXACT = "counts up to 2048 are exact in float16"
FIRST_TOTAL = 5
HEAD_STEPS = H - 1 - FIRST_TOTAL
BANKS = {"out": (7, 4, 5, 6), "mlp_out": (4, 5, 6, 7)}
TOP_BIT = float(1 << (LEVEL - 1))

COLS = {}
_at = 0
for _name, _n in (("bq", H), ("bk", H), ("bv", H), ("ob", C), ("b1", KC), ("b2", C),
                  ("ada_b", 6 * C), ("s", B * NT), ("cond", C * B)):
    COLS[_name] = (_at, _at + _n)
    _at += _n
NCOLS = _at


def bisection_slots():
    places = [("out", u, r) for u in range(1, 4) for r in range(4)][3:-1]
    places += [("mlp_in", u, r) for u in range(4) for r in range(4) if (u or r == 3) and (u == 0 or r)]
    places += [("mlp_out", u, r) for u in range(4) for r in range(4)]
    del places[LEVEL - HEAD_STEPS]
    return {place: HEAD_STEPS + n for n, place in enumerate(places[:STEPS - HEAD_STEPS])}


SLOTS = bisection_slots()
RANK_SLOT = ("mlp_out", 1, 2)
LN1_SLOT = ("mlp_out", 3, 1)
ADA_STEP = 8


def places():
    place = {}
    for q in range(QUAD):
        for j in range(2):
            place[v_half(q, j)] = (0, j)
    for h in range(H):
        place[qk_half(h)] = (1, h % 2)
    for unit in range(NUNIT):
        for j in range(2):
            place[unit_half(unit, j)] = (unit % 2, j)
    return place


def v_half(q, j):
    return j if q == 0 else 4 + 6 * (q - 1) + j


def qk_half(h):
    if h < 2:
        return 2 + h
    if h < 14:
        return 4 + 6 * ((h - 2) // 4) + 2 + (h - 2) % 4
    return 24 + h - 14


def unit_half(unit, j):
    return 22 + j if unit == 0 else NQKV + 2 * unit + j


PLACE = places()


def block_kernel(nc, x, cond, weights, ada_w, cols, out):
    ctx = ExitStack()
    with ctx:
        here = [(nc.sbuf_base + 31) // 32 * 32]

        def at(name, shape, dt, offset):
            return nc.alloc_sbuf_tensor_at(name, shape, dt, offset=offset)

        def room(nbytes):
            offset = here[0]
            here[0] += (nbytes + 31) // 32 * 32
            assert here[0] <= nc.sbuf_usable_end, here[0]
            return offset

        def new(name, shape, dt):
            n = 4 if dt in (F32, F32R, I32) else 2
            for s in shape[1:]:
                n *= s
            return at(name, shape, dt, room(n))

        xm = new("xm", [P, NT, D], F32)
        adj = new("adj", [P, NT, D], F32)
        rank = adj[:, :, :].rearrange("p i d -> p (i d)")
        keys = rank.bitcast(I32)
        keys16 = rank.bitcast(U16).rearrange("p (n s) -> p n s", s=2)
        xT = new("xT", [P, 2, C, T], F32R)
        wraw = new("wraw", [P, 2, HALF], F32)
        w = new("w", [P, 2, 2, 2 * HALF], F32R)
        qk = new("qk", [P, 2, 2, T], F32R)
        act_at = room(2 * KC * T * 4)
        act = at("act", [P, 2, KC, T], F32R, act_at)
        adaw = at("adaw", [P, C, 6 * D], F32, act_at)
        prob_at = room(NT * T * 4)
        prob = at("prob", [P, NT, T], F32, prob_at)
        xr = at("xr", [P, NT, D], F32, prob_at)
        pt_at = room(2 * NT * T * 4)
        probT = at("probT", [P, 2, NT, T], F32R, pt_at)
        low = at("low", [P, NT * T], F32, pt_at)
        eqm = at("eqm", [P, NT * T], BF16, pt_at + NT * T * 4)
        gtm = at("gtm", [P, NT * T], BF16, pt_at + NT * T * 6)
        v_at = room(2 * 2 * NT * T * 4)
        v = at("v", [P, 2, 2, NT, QUAD * DH], F32R, v_at)
        yT = at("yT", [P, C, T], F32, v_at)
        z = at("z", [P, NT, D], F32, v_at + 8192)
        x2 = at("x2", [P, NT, D], F32, v_at + 16384)
        tmp = at("tmp", [P, 4, T], F32, v_at + 24576)
        tb = new("tb", [P, T], F32)
        flip = tb[:, :].bitcast(I32)
        passed_v = tb[:, :].bitcast(BF16)
        passed_s = new("passed_s", [P, NCOUNT], BF16)
        small = new("small", [P, NCOLS], F32)
        ident = new("ident", [P, P], F32)
        ones = new("ones", [P, P], F16)
        minus_half = new("minus_half", [P, P], F16)
        before = new("before", [P, P], F16)
        ada = new("ada", [P, 6 * C, B], F32)
        ada1 = new("ada1", [P, 2 * C], F32)
        ada2 = new("ada2", [P, 4 * C], F32)
        scur = new("scur", [P, NT], F32)
        rowmax = new("rowmax", [P, NT], F32)
        nbias = new("nbias", [P, NT], F32)
        nxmax = new("nxmax", [P, NT], F32)
        nxsum = new("nxsum", [P, NT], F32)
        rowsum = new("rowsum", [P, NT], F32)
        rinv = new("rinv", [P, NT], F32)
        stats = new("stats", [P, NT, 2, 6], F32)
        meanvar = new("meanvar", [P, NT, 2], F32)
        var = new("var", [P, NT], F32)
        std = new("std", [P, NT], F32)
        rstd = new("rstd", [P, NT], F32)
        newt = new("newt", [P, NT], F32)
        cand = new("cand", [P, 1], F32)
        step_up = new("step_up", [P, 1], F32)
        cnt_v = new("cnt_v", [P, 1], F16)
        cnt_s = new("cnt_s", [P, 1], F16)
        n_gt = new("n_gt", [P, 1], F16)
        n_eq = new("n_eq", [P, 1], F16)
        need = new("need", [P, 1], F32)
        rank0 = new("rank0", [P, 1], F32)

        def col(name, i):
            return small[:, COLS[name][0] + i:COLS[name][0] + i + 1]

        bank = [ctx.enter_context(nc.psum_tensor(f"bank{i}", [P, 512], F32)) for i in range(8)]

        def total(step):
            return bank[6 if step < HEAD_STEPS else 3]

        def sem(name):
            return ctx.enter_context(nc.semaphore(name))

        small_in, ada_in, xn_in, tb_in = sem("small_in"), sem("ada_in"), sem("xn_in"), sem("tb_in")
        xr_in = sem("xr_in")
        raw_in = [sem("raw_in0"), sem("raw_in1")]
        ident_zero, consts_ready = sem("ident_zero"), sem("consts_ready")
        w_hi, w_ready = sem("w_hi"), sem("w_ready")
        ada_done = sem("ada_done")
        q_done, k_done, v_done, pv_done = sem("q_done"), sem("k_done"), sem("v_done"), sem("pv_done")
        q_hi, k_hi, v_hi, o_hi = sem("q_hi"), sem("k_hi"), sem("v_hi"), sem("o_hi")
        q_lo, k_lo, v_lo, o_lo = sem("q_lo"), sem("k_lo"), sem("v_lo"), sem("o_lo")
        scores, nbias_ready, exp_done, prob_ready = (sem("scores"), sem("nbias_ready"),
                                                     sem("exp_done"), sem("prob_ready"))
        pt_done, pt_hi, pt_lo = sem("pt_done"), sem("pt_hi"), sem("pt_lo")
        y_done, y_gated, y_back = sem("y_done"), sem("y_gated"), sem("y_back")
        var_ready, std_ready, z_ready = sem("var_ready"), sem("std_ready"), sem("z_ready")
        zt_done, xt_full, xt_hi, xt_lo = sem("zt_done"), sem("xt_full"), sem("xt_hi"), sem("xt_lo")
        f_done, g_done, h_hi, h_lo = sem("f_done"), sem("g_done"), sem("h_hi"), sem("h_lo")
        y2_done, y2_gated, y2_back, out_ready = (sem("y2_done"), sem("y2_gated"), sem("y2_back"),
                                                 sem("out_ready"))
        xmax_ready, xexp_done, adj_ready, diag_done = (sem("xmax_ready"), sem("xexp_done"),
                                                       sem("adj_ready"), sem("diag_done"))
        cand_ready, counted_v, counted_s, total_ready = (sem("cand_ready"), sem("counted_v"),
                                                         sem("counted_s"), sem("total_ready"))
        ties_counted, ranks_ready, xm_ready = sem("ties_counted"), sem("ranks_ready"), sem("xm_ready")
        x_gt_ready = sem("x_gt_ready")
        y2_added = sem("y2_added")
        out_stored = sem("out_stored")
        waits_met = sem("waits_met")

        W_CREDIT = 2
        STORE_CREDIT = 16
        Y2_CREDIT = C

        block = ctx.enter_context(nc.Block())

        x_seq = x.rearrange("b (p i) d -> b p (i d)", p=P)
        out_seq = out.rearrange("b (p i) d -> b p (i d)", p=P)

        def seq(view, b):
            return view[b] if isinstance(b, int) else view[bass.ds(b, 1)].rearrange("a p n -> (a p) n")

        def wait_apart(eng, signal, value):
            eng.wait_ge(signal, value)
            eng.sem_inc(waits_met, 1)

        def w_wait(eng, b, n):
            eng.wait_ge(w_ready, b * NHALF + (n + 1 + W_CREDIT))

        @block.sync
        def _(sp):
            pairs = weights.rearrange("(m s) p n -> m s p n", s=2)

            def load_halves(b, lo, hi):
                with sp.Fori(lo // 2, hi // 2) as m:
                    for slot in range(2):
                        wait_apart(sp, w_ready, b * NHALF + m * 2 + (slot + W_CREDIT - 1))
                        src = pairs[bass.ds(m, 1), slot].rearrange("a p n -> (a p) n")
                        sp.dma_start(wraw[:, slot, :], src).then_inc(raw_in[slot], 16)

            def load_x(b):
                sp.dma_start(rank, seq(x_seq, b)).then_inc(xn_in, 16)
                row = cond[b:b + 1, :] if isinstance(b, int) else cond[bass.ds(b, 1), :]
                sp.dma_start(tb[:, :], row.to_broadcast([P, T])).then_inc(tb_in, 16)

            def load_x_again(b):
                sp.dma_start(xr[:, :, :].rearrange("p i d -> p (i d)"), seq(x_seq, b)).then_inc(xr_in, 16)

            def store(b):
                wait_apart(sp, out_ready, b + 1)
                sp.dma_start(seq(out_seq, b), x2[:, :, :].rearrange("p i d -> p (i d)"))\
                    .then_inc(out_stored, 16)

            def sequence(b, first=False, last=False):
                load_halves(b, 0, 4)
                if not first:
                    store(b - 1)
                load_halves(b, 4, 8)
                if not last:
                    wait_apart(sp, xm_ready, b + 1)
                    load_x(b + 1)
                load_halves(b, 8, NQKV + 6)
                if not last:
                    wait_apart(sp, pt_done, b * (H * NT) + H * NT)
                    load_x_again(b + 1)
                load_halves(b, NQKV + 6, NHALF)

            sp.sem_inc(out_stored, STORE_CREDIT)
            sp.dma_start(small[:, :], cols).then_inc(small_in, 16)
            load_x(0)
            for c in range(C):
                sp.dma_start(adaw[:, c, :], ada_w[c * P:(c + 1) * P, :]).then_inc(ada_in, 16)
            load_x_again(0)
            sequence(0, first=True)
            with sp.Fori(1, B - 1) as b:
                sequence(b)
            sequence(B - 1, last=True)
            store(B - 1)
            sp.wait_ge(out_stored, 16 * B + STORE_CREDIT)

        @block.gpsimd
        def _(pool):
            minus_inf = pool.to_reg(float("-inf"))
            nc.gpsimd.memset(ident[:, :], 0.0).then_inc(ident_zero, 1)
            nc.gpsimd.memset(ones[:, :], 1.0).then_inc(ident_zero, 1)
            nc.gpsimd.memset(minus_half[:, :], -0.5).then_inc(consts_ready, 1)
            pool.wait_ge(ident_zero, 2)
            nc.gpsimd.affine_select(out=ident[:, :], in_=ident[:, :], compare_op=ALU.not_equal, fill=1.0,
                                    base=0, pattern=[[-1, P]], channel_multiplier=1).then_inc(consts_ready, 1)
            nc.gpsimd.affine_select(out=before[:, :], in_=ones[:, :], compare_op=ALU.is_gt, fill=0.0,
                                    base=0, pattern=[[1, P]], channel_multiplier=-1).then_inc(consts_ready, 1)
            pool.sem_inc(w_ready, W_CREDIT)

            def clear_diagonal(t):
                wait_apart(pool, adj_ready, t + 1)
                nc.gpsimd.affine_select(out=adj[:, :, :], in_=adj[:, :, :], compare_op=ALU.not_equal,
                                        fill=minus_inf, base=0, pattern=[[-1, NT], [1, T]],
                                        channel_multiplier=-NT).then_inc(diag_done, 1)

            def split_lo(b, n):
                region, half = PLACE[n]
                span = slice(half * HALF, (half + 1) * HALF)
                pool.wait_ge(w_hi, b * NHALF + (n + 1))
                nc.gpsimd.tensor_tensor(w[:, region, 1, span], wraw[:, n % 2, :],
                                        w[:, region, 0, span].bitcast(F32), ALU.subtract)\
                    .then_inc(w_ready, 1)

            def add_greater(t):
                pool.wait_ge(xr_in, t * 16 + 16)
                x_rows = xr[:, :, :].rearrange("p i d -> p (i d)")
                pool.wait_ge(ties_counted, t + 1)
                nc.gpsimd.tensor_tensor(x_rows, x_rows, gtm[:, :], ALU.add).then_inc(x_gt_ready, 1)

            def sequence(b, last=False):
                for n in range(NHALF):
                    if n == unit_half(NUNIT - 1, 0) and not last:
                        add_greater(b + 1)
                    if n == qk_half(5) and not last:
                        clear_diagonal(b + 1)
                    split_lo(b, n)

            clear_diagonal(0)
            add_greater(0)
            with pool.Fori(0, B - 1) as b:
                sequence(b)
            sequence(B - 1, last=True)

        @block.scalar
        def _(act_e):
            def topk_exp(t):
                for i in range(NT):
                    act_e.wait_ge(xmax_ready, t * NT + (i + 1))
                    ins = nc.scalar.activation(adj[:, i, :], adj[:, i, :], ACT.Exp, bias=nxmax[:, i:i + 1],
                                               accum_out=nxsum[:, i:i + 1])
                ins.then_inc(xexp_done, 1)

            def topk_count(t, step):
                src = keys16[:, NCOUNT:, 1] if step < LEVEL else low[:, NCOUNT:]
                act_e.wait_ge(cand_ready, t * STEPS + (step + 1))
                with nc.allow_low_precision(reason=EXACT):
                    nc.scalar.activation(passed_s[:, :], src, ACT.Sign, bias=cand[:, :], scale=-1.0,
                                         accum_out=cnt_s[:, :]).then_inc(counted_s, 1)

            def ln_root(k):
                act_e.wait_ge(var_ready, k + 1)
                nc.scalar.activation(std[:, :], var[:, :], ACT.Sqrt).then_inc(std_ready, 1)

            def ln_hi(k, shift, scale1):
                for c in range(C):
                    act_e.wait_ge(zt_done, k * C + (c + 1))
                    nc.scalar.activation(tmp[:, c, :], bank[c][:, :], ACT.Identity,
                                         bias=shift[:, c:c + 1], scale=scale1[:, c:c + 1]).then_inc(xt_full, 1)
                    nc.scalar.activation(xT[:, 0, c, :], bank[c][:, :], ACT.Identity,
                                         bias=shift[:, c:c + 1], scale=scale1[:, c:c + 1]).then_inc(xt_hi, 1)

            def split_hi(b, n, freed, count):
                region, half = PLACE[n]
                act_e.wait_ge(freed, count)
                act_e.wait_ge(raw_in[n % 2], b * (16 * NHALF // 2) + 16 * (n // 2 + 1))
                nc.scalar.copy(w[:, region, 0, half * HALF:(half + 1) * HALF], wraw[:, n % 2, :])\
                    .then_inc(w_hi, 1)

            def split_v(b, q, *halves_of_it):
                for j in halves_of_it or (0, 1):
                    if q:
                        split_hi(b, v_half(q, j), v_done, b * H + QUAD * q)
                    else:
                        split_hi(b, v_half(q, j), y2_done, b * C + (Y2_CREDIT - 1))

            def split_qk(b, h):
                if h >= 2:
                    split_hi(b, qk_half(h), k_done, b * H + (h - 1))
                else:
                    split_hi(b, qk_half(h), y2_done, b * C + Y2_CREDIT)

            def split_unit(b, u, *halves_of_it):
                for half in halves_of_it or (0, 1):
                    n = unit_half(u, half)
                    if u == 0:
                        split_hi(b, n, v_done, b * H + H)
                    elif u == 1:
                        split_hi(b, n, k_done, b * H + H)
                    elif u < 6:
                        split_hi(b, n, y_done, b * C + (u - 1))
                    elif u < 10:
                        split_hi(b, n, f_done, b * KC + 4 * (u - 5))
                    else:
                        split_hi(b, n, y2_done, b * C + (Y2_CREDIT + u - 9))

            def v_part(b, idx):
                act_e.wait_ge(v_done, b * H + (idx + 1))
                if idx == QUAD:
                    act_e.wait_ge(out_stored, b * 16 + STORE_CREDIT)
                bk = bank[4 + idx] if idx < 4 else bank[7]
                nc.scalar.copy(v[:, (idx // 4) % 2, 0, idx % 4, :], bk[:, :]).then_inc(v_hi, 1)

            def qk_part(b, h):
                act_e.wait_ge(q_done, b * H + (h + 1))
                nc.scalar.activation(qk[:, 0, 0, :], bank[4 if h else 1][:, :], ACT.Identity,
                                     bias=col("bq", h))\
                    .then_inc(q_hi, 1)
                act_e.wait_ge(k_done, b * H + (h + 1))
                nc.scalar.activation(qk[:, 1, 0, :], bank[5 if h else 2][:, :], ACT.Identity,
                                     bias=col("bk", h))\
                    .then_inc(k_hi, 1)

            def head(b, h, last):
                for i in range(NT):
                    act_e.wait_ge(nbias_ready, b * (H * NT) + (h * NT + i + 1))
                    nc.scalar.activation(prob[:, i, :], bank[i][:, :], ACT.Exp, bias=nbias[:, i:i + 1],
                                         scale=SCALE, accum_out=rowsum[:, i:i + 1]).then_inc(exp_done, 1)
                if h + 1 < H:
                    qk_part(b, h + 1)
                if h + 2 < H:
                    split_qk(b, h + 2)
                else:
                    split_unit(b, 1, h - (H - 2))
                for j in range(NT):
                    act_e.wait_ge(pt_done, b * (H * NT) + (h * NT + j + 1))
                    nc.scalar.copy(probT[:, 0, j, :], bank[j][:, :]).then_inc(pt_hi, 1)
                if FIRST_TOTAL <= h + 1 < H and not last:
                    topk_count(b + 1, h + 1 - FIRST_TOTAL)
                if h + QUAD < H:
                    v_part(b, h + QUAD)
                if h == 0 and not last:
                    topk_exp(b + 1)
                refill(b, h, 0)
                act_e.wait_ge(pv_done, b * H + (h + 1))
                nc.scalar.activation(act[:, 0, h, :], bank[6][:, :], ACT.Identity, bias=col("bv", h))\
                    .then_inc(o_hi, 1)
                refill(b, h, 1)

            def refill(b, h, half):
                if h in (3, 7):
                    split_v(b, h // QUAD + 2, half)
                elif h == 11:
                    split_unit(b, 0, half)

            def sequence(b, last=False):
                split_qk(b, 0)
                split_qk(b, 1)
                for idx in range(3):
                    v_part(b, idx)
                qk_part(b, 0)
                v_part(b, 3)
                split_v(b, 1)
                for h in range(H):
                    head(b, h, last)

                def next_count(place):
                    step = SLOTS.get(place)
                    if not last and step is not None and step + 1 < STEPS:
                        topk_count(b + 1, step + 1)

                split_unit(b, 2, 0)
                next_count(("out", 1, 3))
                split_unit(b, 2, 1)
                for u in (2, 3):
                    for r in range(4):
                        next_count(("out", u, r))
                        if r % 2 == 0:
                            split_unit(b, u + 1, r // 2)
                ln_root(b * 2 + 1)
                split_unit(b, 5, 0)
                ln_hi(b * 2 + 1, ada2[:, C:2 * C], ada2[:, 2 * C:3 * C])
                split_unit(b, 5, 1)
                for f in range(KC):
                    next_count(("mlp_in", f // 4, f % 4))
                    act_e.wait_ge(f_done, b * KC + (f + 1))
                    if f >= 4:
                        act_e.wait_ge(h_lo, b * KC + (f - 3))
                    nc.scalar.activation(tmp[:, f % 4, :], bank[4 + f % 4][:, :], ACT.Gelu,
                                         bias=col("b1", f)).then_inc(g_done, 1)
                    nc.scalar.activation(act[:, 0, f, :], bank[4 + f % 4][:, :], ACT.Gelu,
                                         bias=col("b1", f)).then_inc(h_hi, 1)
                    if f % 4 == 3:
                        split_unit(b, 6 + f // 4, 0)
                    elif f % 4 == 1 and f > 4:
                        split_unit(b, 5 + f // 4, 1)
                for u in range(4):
                    for r in range(4):
                        next_count(("mlp_out", u, r))
                        if r == 1 and u < 3:
                            split_unit(b, 9 + u, 1)
                        elif r == 3 and u < 2:
                            split_unit(b, 10 + u, 0)
                            if u == 1 and not last:
                                ln_root(b * 2 + 2)
                        elif not last and (u, r) in ((2, 3), (3, 1)):
                            split_v(b + 1, 0, u - 2)
                if not last:
                    ln_hi(b * 2 + 2, ada1[:, 0:C], ada1[:, C:2 * C])

            act_e.wait_ge(small_in, 16)
            topk_exp(0)
            for step in range(STEPS):
                topk_count(0, step)
            split_v(0, 0)
            ln_root(0)
            ln_hi(0, ada1[:, 0:C], ada1[:, C:2 * C])
            with act_e.Fori(0, B - 1) as b:
                sequence(b)
            sequence(B - 1, last=True)

        @block.vector
        def _(dve):
            V = nc.vector

            def count(t, step):
                src = keys16[:, :NCOUNT, 1] if step < LEVEL else low[:, :NCOUNT]
                with nc.allow_low_precision(reason=EXACT):
                    V.tensor_scalar(passed_v, src, cand[:, :], None, op0=ALU.is_ge, op1=ALU.add,
                                    accum_out=cnt_v[:, :]).then_inc(counted_v, 1)

            def start_level(t, step):
                V.memset(cand[:, :], TOP_BIT - 0.5).then_inc(cand_ready, 1)
                dve.drain()
                count(t, step)

            def topk_rowmax(t):
                dve.wait_ge(xn_in, t * 16 + 16)
                for i in range(NT):
                    V.tensor_reduce(nxmax[:, i:i + 1], adj[:, i, :], AX.X, ALU.max, negate=True)\
                        .then_inc(xmax_ready, 1)
                if isinstance(t, int):
                    dve.wait_ge(small_in, 16)
                src = small[:, COLS["s"][0]:COLS["s"][1]].rearrange("p (b i) -> p b i", b=B)
                V.tensor_copy(scur[:, :], src[:, t, :] if isinstance(t, int) else
                              src[:, bass.ds(t, 1), :].rearrange("p a i -> p (a i)"))

            def topk_softmax(t):
                dve.wait_ge(xexp_done, t + 1)
                V.reciprocal(rinv[:, :], nxsum[:, :])
                dve.drain()
                for i in range(NT):
                    V.tensor_scalar(adj[:, i, :], adj[:, i, :], rinv[:, i:i + 1], float(np.float32(T ** -0.5)),
                                    ALU.mult, ALU.mult)

            def topk_adj(t):
                dve.drain()
                dve.wait_ge(tb_in, t * 16 + 16)
                for i in range(NT):
                    ins = V.scalar_tensor_tensor(adj[:, i, :], tb[:, :], scur[:, i:i + 1], adj[:, i, :],
                                                 ALU.mult, ALU.mult)
                ins.then_inc(adj_ready, 1)

            def topk_keys(t, lo, hi):
                if lo == 0:
                    dve.wait_ge(diag_done, t + 1)
                for i in range(lo, hi):
                    part = keys[:, i * T:(i + 1) * T]
                    V.tensor_scalar(flip, part, 31, -(1 << 31), ALU.arith_shift_right, ALU.bitwise_or)
                    dve.drain()
                    V.tensor_tensor(part, part, flip, ALU.bitwise_xor)
                    dve.drain()

            def topk_step(t, step):
                topk_move(t, step)
                if step % LEVEL != LEVEL - 1:
                    count(t, step + 1)

            def topk_move(t, step):
                dve.wait_ge(total_ready, t * STEPS + (step + 1))
                bit = TOP_BIT / (1 << step % LEVEL)
                V.tensor_scalar(step_up[:, :], total(step)[:, 0:1], float(KTOP - P * NCOUNT // 2) - 0.5, bit,
                                ALU.is_gt, ALU.mult)
                dve.drain()
                move = V.scalar_tensor_tensor(cand[:, :], step_up[:, :], -bit / 2, cand[:, :], ALU.add, ALU.add)
                if step % LEVEL != LEVEL - 1:
                    move.then_inc(cand_ready, 1)
                dve.drain()
                if step == LEVEL - 1:
                    V.tensor_scalar(low[:, :], keys16[:, :, 1], cand[:, :], float(1 << 17),
                                    ALU.subtract, ALU.mult)
                    dve.drain()
                    V.tensor_tensor(low[:, :], low[:, :], keys16[:, :, 0], ALU.add)
                    dve.drain()
                    start_level(t, step + 1)
                elif step == STEPS - 1:
                    with nc.allow_low_precision(reason=EXACT):
                        V.tensor_scalar(eqm[:, :], low[:, :], cand[:, :], None, op0=ALU.is_equal, op1=ALU.add,
                                        accum_out=n_eq[:, :])
                        V.tensor_scalar(gtm[:, :], low[:, :], cand[:, :], None, op0=ALU.is_gt, op1=ALU.add,
                                        accum_out=n_gt[:, :]).then_inc(ties_counted, 1)

            def topk_mask(t):
                dve.wait_ge(ranks_ready, t + 1)
                V.tensor_scalar(need[:, :], bank[3][:, 0:1], -1.0, float(KTOP), ALU.mult, ALU.add)
                V.tensor_copy(rank0[:, :], bank[3][:, 1:2])
                dve.drain()
                V.tensor_tensor_scan(rank, eqm[:, :], eqm[:, :], rank0[:, :], ALU.add, ALU.max)
                dve.drain()
                V.scalar_tensor_tensor(eqm[:, :], rank, need[:, :], eqm[:, :], ALU.is_le, ALU.mult)
                dve.drain()
                dve.wait_ge(x_gt_ready, t + 1)
                V.tensor_tensor(xm[:, :, :].rearrange("p i d -> p (i d)"),
                                xr[:, :, :].rearrange("p i d -> p (i d)"), eqm[:, :], ALU.add)\
                    .then_inc(xm_ready, 1)
                dve.drain()

            def row_stats(src, part, lo, hi):
                for i in range(NT):
                    V.bn_stats(stats[:, i, part, :], src[:, i, lo:hi])

            def normalise(k, src, parts):
                dve.drain()
                for i in range(NT):
                    V.bn_aggr(meanvar[:, i, :], stats[:, i, 0:parts, :].rearrange("p a s -> p (a s)"))
                dve.drain()
                V.tensor_scalar(var[:, :], meanvar[:, :, 1], EPS, None, ALU.add).then_inc(var_ready, 1)
                dve.wait_ge(std_ready, k + 1)
                V.reciprocal(rstd[:, :], std[:, :])
                dve.drain()
                V.tensor_tensor(newt[:, :], rstd[:, :], rstd[:, :], ALU.mult)
                dve.drain()
                V.scalar_tensor_tensor(newt[:, :], newt[:, :], -0.5, var[:, :], ALU.mult, ALU.mult)
                dve.drain()
                V.scalar_tensor_tensor(rstd[:, :], newt[:, :], 1.5, rstd[:, :], ALU.add, ALU.mult)
                dve.drain()
                for i in range(NT):
                    V.tensor_scalar(z[:, i, :], src[:, i, :], meanvar[:, i, 0:1], rstd[:, i:i + 1],
                                    ALU.subtract, ALU.mult).then_inc(z_ready, 1)

            def modulate_lo(k):
                for c in range(C):
                    dve.wait_ge(xt_full, k * C + (c + 1))
                    dve.wait_ge(xt_hi, k * C + (c + 1))
                    V.tensor_tensor(xT[:, 1, c, :], tmp[:, c, :], xT[:, 0, c, :].bitcast(F32), ALU.subtract)\
                        .then_inc(xt_lo, 1)

            def v_part(b, idx):
                dve.wait_ge(v_hi, b * H + (idx + 1))
                bk = bank[4 + idx] if idx < 4 else bank[7]
                V.tensor_tensor(v[:, (idx // 4) % 2, 1, idx % 4, :], bk[:, :],
                                v[:, (idx // 4) % 2, 0, idx % 4, :].bitcast(F32), ALU.subtract).then_inc(v_lo, 1)

            def biased_lo(dst, src, bias, hi):
                return V.scalar_tensor_tensor(dst, src, bias, hi.bitcast(F32), ALU.add, ALU.subtract)

            def qk_part(b, h):
                dve.wait_ge(q_hi, b * H + (h + 1))
                biased_lo(qk[:, 0, 1, :], bank[4 if h else 1][:, :], col("bq", h), qk[:, 0, 0, :]).then_inc(q_lo, 1)
                dve.wait_ge(k_hi, b * H + (h + 1))
                biased_lo(qk[:, 1, 1, :], bank[5 if h else 2][:, :], col("bk", h), qk[:, 1, 0, :]).then_inc(k_lo, 1)

            def topk_under_head(t, h):
                if h == 0:
                    topk_rowmax(t)
                elif h == 1:
                    topk_softmax(t)
                elif h == 2:
                    topk_adj(t)
                elif h == 3:
                    topk_keys(t, 0, 3)
                elif h == 4:
                    topk_keys(t, 3, NT)
                    start_level(t, 0)
                elif h < H - 1 and h >= FIRST_TOTAL:
                    count(t, h + 1 - FIRST_TOTAL)

            def head(b, h, last):
                tile = h * NT
                for i in range(NT + 1):
                    if i < NT:
                        dve.wait_ge(scores, b * (H * NT) + (tile + i + 1))
                        V.reduce_max(rowmax[:, i:i + 1], bank[i][:, :], AX.X)
                    if i:
                        dve.wait_ge(exp_done, b * (H * NT) + (tile + i))
                        V.reciprocal(rinv[:, i - 1:i], rowsum[:, i - 1:i])
                    dve.drain()
                    if i < NT:
                        V.tensor_scalar(nbias[:, i:i + 1], rowmax[:, i:i + 1], -SCALE, None, ALU.mult)\
                            .then_inc(nbias_ready, 1)
                    if i:
                        V.tensor_scalar(prob[:, i - 1, :], prob[:, i - 1, :], rinv[:, i - 1:i], None, ALU.mult)\
                            .then_inc(prob_ready, 1)
                if FIRST_TOTAL <= h < H - 1 and not last:
                    topk_move(b + 1, h - FIRST_TOTAL)
                if h + 1 < H:
                    qk_part(b, h + 1)
                for j in range(NT):
                    dve.wait_ge(pt_hi, b * (H * NT) + (tile + j + 1))
                    V.tensor_tensor(probT[:, 1, j, :], bank[j][:, :], probT[:, 0, j, :].bitcast(F32),
                                    ALU.subtract).then_inc(pt_lo, 1)
                if not last:
                    topk_under_head(b + 1, h)
                if h + QUAD < H:
                    v_part(b, h + QUAD)
                dve.wait_ge(o_hi, b * H + (h + 1))
                biased_lo(act[:, 1, h, :], bank[6][:, :], col("bv", h), act[:, 0, h, :]).then_inc(o_lo, 1)

            def gate(done, gated, b, u, bias, gates, banks):
                dve.wait_ge(done, b * C + (u + 1 + (Y2_CREDIT if done is y2_done else 0)))
                V.tensor_scalar(yT[:, u, :], bank[banks[u]][:, :], col(bias, u), gates[:, u:u + 1],
                                ALU.add, ALU.mult).then_inc(gated, 1)

            def hidden_lo(b, f):
                dve.wait_ge(h_hi, b * KC + (f + 1))
                V.tensor_tensor(act[:, 1, f, :], tmp[:, f % 4, :], act[:, 0, f, :].bitcast(F32),
                                ALU.subtract).then_inc(h_lo, 1)

            def sequence(b, last=False):
                src = ada[:, 2 * C:6 * C, b] if isinstance(b, int) else \
                    ada[:, 2 * C:6 * C, bass.ds(b, 1)].rearrange("p c a -> p (c a)")
                V.tensor_copy(ada2[:, :], src)
                for idx in range(3):
                    v_part(b, idx)
                qk_part(b, 0)
                v_part(b, 3)
                for h in range(H):
                    head(b, h, last)

                def step_at(place):
                    if not last and place in SLOTS:
                        topk_step(b + 1, SLOTS[place])

                def attn_gate(u):
                    gate(y_done, y_gated, b, u, "ob", ada2[:, 0:C], BANKS["out"])

                def mlp_gate(u):
                    gate(y2_done, y2_gated, b, u, "b2", ada2[:, 3 * C:4 * C], BANKS["mlp_out"])

                def add_back(back, base, u):
                    dve.wait_ge(back, b * C + (u + 1))
                    part = slice(u * P, (u + 1) * P)
                    return V.tensor_tensor(x2[:, :, part], base[:, :, part],
                                           bank[u][:, :].rearrange("p (i j) -> p i j", i=NT), ALU.add)

                attn_gate(0)
                step_at(("out", 1, 3))
                attn_gate(1)
                for u in (2, 3):
                    for r in range(4):
                        if u == 3 and r == 0:
                            attn_gate(2)
                        step_at(("out", u, r))
                        if u == 2 and r == 1:
                            add_back(y_back, xm, 0)
                        if r == 2:
                            add_back(y_back, xm, u - 1)
                attn_gate(3)
                dve.drain()
                row_stats(x2, 0, 0, 3 * P)
                add_back(y_back, xm, 3)
                dve.drain()
                row_stats(x2, 1, 3 * P, D)
                normalise(b * 2 + 1, x2, 2)
                modulate_lo(b * 2 + 1)
                V.tensor_tensor(x2[:, :, :].rearrange("p i d -> p (i d)"),
                                x2[:, :, :].rearrange("p i d -> p (i d)"),
                                xm[:, :, :].rearrange("p i d -> p (i d)"), ALU.add)
                for f in range(KC):
                    step_at(("mlp_in", f // 4, f % 4))
                    if f:
                        hidden_lo(b, f - 1)
                hidden_lo(b, KC - 1)
                for u in range(4):
                    for r in range(4):
                        if u and r == 0:
                            mlp_gate(u - 1)
                        step_at(("mlp_out", u, r))
                        if (u, r) == (1, 2):
                            add_back(y2_back, x2, 0)
                        if u == 3 and r == 0:
                            add_back(y2_back, x2, 1)
                            add_back(y2_back, x2, 2).then_inc(y2_added, 1)
                        if not last and ("mlp_out", u, r) == RANK_SLOT:
                            topk_mask(b + 1)
                            next_modulation(b + 1)
                            row_stats(xm, 0, 0, D)
                            normalise(b * 2 + 2, xm, 1)
                if not last:
                    modulate_lo(b * 2 + 2)
                mlp_gate(3)
                add_back(y2_back, x2, 3).then_inc(out_ready, 1)

            def next_modulation(t):
                src = ada[:, 0:2 * C, t] if isinstance(t, int) else \
                    ada[:, 0:2 * C, bass.ds(t, 1)].rearrange("p c a -> p (c a)")
                V.tensor_copy(ada1[:, :], src)

            topk_rowmax(0)
            topk_softmax(0)
            topk_adj(0)
            topk_keys(0, 0, NT)
            start_level(0, 0)
            for step in range(STEPS):
                topk_step(0, step)
            dve.wait_ge(ada_done, 1)
            ada_b = small[:, COLS["ada_b"][0]:COLS["ada_b"][1]]
            V.tensor_tensor(ada[:, :, :], bank[0][:, 0:6 * C * B].rearrange("p (m b) -> p m b", b=B),
                            ada_b.unsqueeze(2).to_broadcast([P, 6 * C, B]), ALU.add)
            dve.drain()
            for part in (1, 4):
                V.tensor_scalar(ada[:, part * C:(part + 1) * C, :], ada[:, part * C:(part + 1) * C, :],
                                1.0, None, ALU.add)
            dve.drain()
            next_modulation(0)
            topk_mask(0)
            row_stats(xm, 0, 0, D)
            normalise(0, xm, 1)
            modulate_lo(0)
            V.memset(newt[:, :], 0.0).then_inc(o_lo, 1)
            with dve.Fori(0, B - 1) as b:
                sequence(b)
            sequence(B - 1, last=True)

        @block.tensor
        def _(pe):
            def mm3(dst, w_hi_ap, w_lo_ap, x_hi_ap, x_lo_ap, first, last):
                pe.matmul(dst, w_hi_ap, x_hi_ap, start=first, stop=False)
                pe.matmul(dst, w_hi_ap, x_lo_ap, start=False, stop=False)
                return pe.matmul(dst, w_lo_ap, x_hi_ap, start=False, stop=last)

            def take_total(t, step):
                pe.wait_ge(counted_v, t * STEPS + (step + 1))
                pe.wait_ge(counted_s, t * STEPS + (step + 1))
                pe.matmul(total(step)[:, 0:1], ones[:, :], cnt_v[:, :], start=True, stop=False)
                pe.matmul(total(step)[:, 0:1], minus_half[:, :], cnt_s[:, :], start=False, stop=True)\
                    .then_inc(total_ready, 1)

            def take_ranks(t):
                pe.wait_ge(ties_counted, t + 1)
                pe.matmul(bank[3][:, 0:1], ones[:, :], n_gt[:, :], start=True, stop=True)
                pe.matmul(bank[3][:, 1:2], before[:, :], n_eq[:, :], start=True, stop=True)\
                    .then_inc(ranks_ready, 1)

            def transpose_z(k):
                for i in range(NT):
                    pe.wait_ge(z_ready, k * NT + (i + 1))
                    for c in range(C):
                        ins = pe.transpose(bank[c][:, i * P:(i + 1) * P], z[:, i, c * P:(c + 1) * P], ident[:, :])
                        if i == NT - 1:
                            ins.then_inc(zt_done, 1)

            def v_mm(bk, m, c):
                part, rows = slice(c * T, (c + 1) * T), slice(m * P, (m + 1) * P)
                return mm3(bk[:, :], xT[:, 0, c, rows], xT[:, 1, c, rows], w[:, 0, 0, part], w[:, 0, 1, part],
                           c == 0, c == C - 1)

            def first_v_tiles(b):
                for c in range(C):
                    if c % 2 == 0:
                        w_wait(pe, b, v_half(0, c // 2))
                    pe.wait_ge(xt_lo, b * (2 * C) + (c + 1))
                    for m in range(NT - 1):
                        ins = v_mm(bank[4 + m], m, c)
                        if c == C - 1:
                            ins.then_inc(v_done, 1)

            def v_tile(b, idx):
                q, m = idx // 4, idx % 4
                if idx >= QUAD:
                    pe.wait_ge(v_lo, b * H + idx)
                for c in range(C):
                    if m == 0 and c % 2 == 0:
                        w_wait(pe, b, v_half(q, c // 2))
                    ins = v_mm(bank[7], m, c)
                ins.then_inc(v_done, 1)

            def qk_proj(b, h):
                w_wait(pe, b, qk_half(h))
                for which, done in ((0, q_done), (1, k_done)):
                    bk = bank[(4 if h else 1) + which]
                    if h == 1:
                        pe.wait_ge(v_lo, b * H + (which + 1))
                    for c in range(C):
                        part = slice((h % 2) * HALF + c * 2 * P + which * P, (h % 2) * HALF + c * 2 * P + which * P + P)
                        ins = mm3(bk[:, :], w[:, 1, 0, part], w[:, 1, 1, part], xT[:, 0, c, :], xT[:, 1, c, :],
                                  c == 0, c == C - 1)
                    ins.then_inc(done, 1)

            def head(b, h, last):
                pe.wait_ge(q_lo, b * H + (h + 1))
                pe.wait_ge(k_lo, b * H + (h + 1))
                for i in range(NT):
                    rows = slice(i * P, (i + 1) * P)
                    mm3(bank[i][:, :], qk[:, 0, 0, rows], qk[:, 0, 1, rows], qk[:, 1, 0, :], qk[:, 1, 1, :],
                        True, True).then_inc(scores, 1)
                step = h - FIRST_TOTAL
                if 0 <= step < HEAD_STEPS and not last:
                    pe.wait_ge(o_lo, b * H + (h + 1))
                    take_total(b + 1, step)
                if h + 1 < H:
                    qk_proj(b, h + 1)
                if h == H - 1:
                    wide(b, "out", 0, 9, KC - 1, y_done)
                    wide(b, "out", 1, 0, 6, y_done)
                pe.wait_ge(prob_ready, b * (H * NT) + (h * NT + NT))
                for j in range(NT):
                    for i in range(NT):
                        ins = pe.transpose(bank[j][:, i * P:(i + 1) * P], prob[:, i, j * P:(j + 1) * P], ident[:, :])
                    ins.then_inc(pt_done, 1)
                if h + QUAD < H:
                    v_tile(b, h + QUAD)
                elif h < H - 1:
                    wide(b, "out", 0, 3 * (h + QUAD - H), 3 * (h + QUAD - H) + 3, y_done)
                else:
                    wide(b, "out", 1, 6, 8, y_done)
                q, m = h // QUAD, h % QUAD
                if m == 0:
                    pe.wait_ge(v_lo, b * H + 4 * (q + 1))
                pe.wait_ge(o_lo, b * H + (h + 1))
                if 0 <= step < HEAD_STEPS and not last:
                    pe.wait_ge(cand_ready, (b + 1) * STEPS + (step + 2))
                for j in range(NT):
                    pe.wait_ge(pt_lo, b * (H * NT) + (h * NT + j + 1))
                    part = slice(m * P, (m + 1) * P)
                    ins = mm3(bank[6][:, :], v[:, q % 2, 0, j, part], v[:, q % 2, 1, j, part],
                              probT[:, 0, j, :], probT[:, 1, j, :], j == 0, j == NT - 1)
                ins.then_inc(pv_done, 1)

            def transpose_back(b, u, gated, back):
                pe.wait_ge(gated, b * C + (u + 1))
                for i in range(NT):
                    ins = pe.transpose(bank[u][:, i * P:(i + 1) * P], yT[:, u, i * P:(i + 1) * P], ident[:, :])
                ins.then_inc(back, 1)

            def wide(b, phase, u, lo, hi, done):
                unit = (0 if phase == "out" else 8) + u
                for kc in range(lo, hi):
                    if kc % 8 == 0:
                        w_wait(pe, b, unit_half(unit, kc // 8))
                    if phase == "out" and kc >= KC - 2:
                        pe.wait_ge(o_lo, b * H + (kc + 2))
                    if phase == "mlp_out" and kc == 0:
                        pe.wait_ge(h_hi, b * KC + (KC - 3 + u))
                    if phase == "mlp_out" and u == 0 and (kc % 4 == 0 or kc == KC - 1):
                        pe.wait_ge(h_lo, b * KC + (KC if kc == KC - 1 else min(kc + 4, KC - 1)))
                    part = slice(kc * P, (kc + 1) * P)
                    ins = mm3(bank[BANKS[phase][u]][:, :], w[:, unit % 2, 0, part], w[:, unit % 2, 1, part],
                              act[:, 0, kc, :], act[:, 1, kc, :], kc == 0, kc == KC - 1)
                    if kc == KC - 1:
                        ins.then_inc(done, 1)

            def between(b, place, last):
                if last:
                    return
                if place in SLOTS:
                    take_total(b + 1, SLOTS[place])
                if place == RANK_SLOT:
                    take_ranks(b + 1)
                if place == LN1_SLOT:
                    pe.wait_ge(y2_added, b + 1)
                    transpose_z(b * 2 + 2)

            def mlp_in(b, last):
                def mm(f, c):
                    unit = 4 + f // 4
                    part = slice(c * T + (f % 4) * P, c * T + (f % 4 + 1) * P)
                    return mm3(bank[4 + f % 4][:, :], w[:, unit % 2, 0, part], w[:, unit % 2, 1, part],
                               xT[:, 0, c, :], xT[:, 1, c, :], c == 0, c == C - 1)

                for c in range(C):
                    if c % 2 == 0:
                        w_wait(pe, b, unit_half(4, c // 2))
                    pe.wait_ge(xt_lo, b * (2 * C) + (C + c + 1))
                    for f in range(4):
                        ins = mm(f, c)
                        if c == C - 1:
                            ins.then_inc(f_done, 1)
                    between(b, ("mlp_in", 0, c), last)
                for f in range(4, KC):
                    pe.wait_ge(h_hi, b * KC + (f - 3))
                    for c in range(C):
                        if f % 4 == 0 and c % 2 == 0:
                            w_wait(pe, b, unit_half(4 + f // 4, c // 2))
                        ins = mm(f, c)
                    ins.then_inc(f_done, 1)
                    between(b, ("mlp_in", f // 4, f % 4), last)

            def sequence(b, last=False):
                first_v_tiles(b)
                qk_proj(b, 0)
                v_tile(b, 3)
                for h in range(H):
                    head(b, h, last)
                wide(b, "out", 1, 8, 11, y_done)
                wide(b, "out", 0, KC - 1, KC, y_done)
                wide(b, "out", 1, 11, KC, y_done)
                between(b, ("out", 1, 3), last)
                for u in (2, 3):
                    for r in range(4):
                        wide(b, "out", u, 4 * r, 4 * r + 4, y_done)
                        if u == 2 and r == 0:
                            transpose_back(b, 0, y_gated, y_back)
                        if r == 1:
                            transpose_back(b, u - 1, y_gated, y_back)
                        between(b, ("out", u, r), last)
                transpose_back(b, 3, y_gated, y_back)
                transpose_z(b * 2 + 1)
                mlp_in(b, last)
                for u in range(4):
                    for r in range(4):
                        wide(b, "mlp_out", u, 4 * r, 4 * r + 4, y2_done)
                        if (u, r) == (1, 1):
                            transpose_back(b, 0, y2_gated, y2_back)
                        elif (u, r) == (3, 0):
                            transpose_back(b, 1, y2_gated, y2_back)
                            transpose_back(b, 2, y2_gated, y2_back)
                        between(b, ("mlp_out", u, r), last)
                if not last:
                    pe.wait_ge(xt_lo, b * (2 * C) + 3 * C)
                transpose_back(b, 3, y2_gated, y2_back)

            pe.sem_inc(y2_done, Y2_CREDIT)
            pe.wait_ge(consts_ready, 3)
            c0 = COLS["cond"][0]
            for step in range(STEPS):
                take_total(0, step)
                if step == ADA_STEP:
                    pe.wait_ge(small_in, 16)
                    pe.wait_ge(ada_in, 16 * C)
                if step >= ADA_STEP:
                    m = step - ADA_STEP
                    for c in range(C):
                        ins = pe.matmul(bank[0][:, m * B:(m + 1) * B], adaw[:, c, m * P:(m + 1) * P],
                                        small[:, c0 + c * B:c0 + (c + 1) * B], start=c == 0, stop=c == C - 1)
            ins.then_inc(ada_done, 1)
            take_ranks(0)
            transpose_z(0)
            with pe.Fori(0, B - 1) as b:
                sequence(b)
            sequence(B - 1, last=True)


def _half_units(qkv_w, out_w, w1, w2):
    n = H * DH
    q = qkv_w.reshape(C, P, 3 * n)

    def pack(a):
        return a.transpose(1, 0, 2).reshape(P, -1)

    halves = np.empty((NHALF, P, HALF), qkv_w.dtype)
    for h in range(H):
        one = np.concatenate([q[:, :, h * DH:(h + 1) * DH], q[:, :, n + h * DH:n + (h + 1) * DH]], axis=2)
        halves[qk_half(h)] = pack(one)
    for g in range(H // QUAD):
        one = pack(q[:, :, 2 * n + g * QUAD * DH:2 * n + (g + 1) * QUAD * DH])
        halves[v_half(g, 0)], halves[v_half(g, 1)] = one[:, :HALF], one[:, HALF:]
    for u in range(4):
        units = (pack(out_w.reshape(KC, P, D)[:, :, u * P:(u + 1) * P]),
                 pack(w1.reshape(C, P, F)[:, :, u * T:(u + 1) * T]),
                 pack(w2.reshape(KC, P, D)[:, :, u * P:(u + 1) * P]))
        for layer, one in enumerate(units):
            for j in range(2):
                halves[unit_half(4 * layer + u, j)] = one[:, j * HALF:(j + 1) * HALF]
    return halves


def kernel(x, fside_BxSx1_0, cond_2048, L1_cond_ada_w, L1_cond_ada_b, L1_cond_qkv_w, L1_cond_qkv_b,
           L1_cond_out_w, L1_cond_out_b, L1_cond_ffn_w1, L1_cond_ffn_b1, L1_cond_ffn_w2, L1_cond_ffn_b2):
    import concourse.bacc as bacc
    from concourse.bass_utils import run_bass_kernel_spmd

    x, s, cond, ada_w, ada_b, qkv_w, qkv_b, out_w, out_b, w1, b1, w2, b2 = (
        np.asarray(a) for a in (x, fside_BxSx1_0, cond_2048, L1_cond_ada_w, L1_cond_ada_b, L1_cond_qkv_w,
                                L1_cond_qkv_b, L1_cond_out_w, L1_cond_out_b, L1_cond_ffn_w1, L1_cond_ffn_b1,
                                L1_cond_ffn_w2, L1_cond_ffn_b2))

    def columns(a):
        return a.reshape(-1, P).T

    cols = np.concatenate([
        columns(qkv_b), columns(out_b), columns(b1), columns(b2), columns(ada_b),
        s.reshape(B, P, NT).transpose(1, 0, 2).reshape(P, B * NT),
        cond.reshape(B, C, P).transpose(2, 1, 0).reshape(P, C * B)], axis=1)
    arrays = {"x_in": np.ascontiguousarray(x), "cond_in": np.ascontiguousarray(cond),
              "weights_in": _half_units(qkv_w, out_w, w1, w2), "ada_w_in": np.ascontiguousarray(ada_w),
              "cols_in": np.ascontiguousarray(cols)}
    nc = bacc.Bacc("TRN2", target_bir_lowering=False, num_devices=1)
    args = [nc.dram_tensor(name, a.shape, mybir.dt.from_np(a.dtype), kind="ExternalInput").ap()
            for name, a in arrays.items()]
    out = nc.dram_tensor("out", (B, T, D), F32, kind="ExternalOutput").ap()
    block_kernel(nc, *args, out)
    return run_bass_kernel_spmd(nc, [arrays], core_ids=[0]).results[0]["out"]
```

```python
from contextlib import ExitStack

import numpy as np

import concourse.bass as bass
from concourse import mybir

F32 = mybir.dt.float32
F32R = mybir.dt.float32r
I32 = mybir.dt.int32
U16 = mybir.dt.uint16
BF16 = mybir.dt.bfloat16
F16 = mybir.dt.float16
ALU = mybir.AluOpType
ACT = mybir.ActivationFunctionType
AX = mybir.AxisListType

P = 128
B, T, D = 4, 512, 512
H, DH = 16, 128
F = 2048
KTOP = 5120
EPS = 1e-6
SCALE = DH ** -0.5
C = D // P
NT = T // P
KC = F // P
HALF = 1024
QUAD = 4
NHALF = 48
NQKV = 24
NUNIT = 12
STEPS = 32
LEVEL = 16
NCOUNT = T * T // P // 2
EXACT = "counts up to 2048 are exact in float16"
FIRST_TOTAL = 5
HEAD_STEPS = H - FIRST_TOTAL
ROWS = (slice(0, T // 2), slice(T // 2, T))
Y_PIECES = C + 1
LNS = 3
BANKS = {"out": (7, 4, 5, 6, 7), "mlp_out": (4, 5, 6, 7)}
TOP_BIT = float(1 << (LEVEL - 1))

COLS = {}
_at = 0
for _name, _n in (("bq", H), ("bk", H), ("bv", H), ("ob", C), ("b1", KC), ("b2", C),
                  ("ada_b", 6 * C), ("s", B * NT), ("cond", C * B)):
    COLS[_name] = (_at, _at + _n)
    _at += _n
NCOLS = _at


def bisection_slots():
    places = [("out", u, r) for u in range(1, 4) for r in range(4)][2:-4]
    places += [("mlp_in", u, r) for u in range(4) for r in range(4) if (u or r == 3) and (u < 3 or r)]
    places += [("mlp_out", u, r) for u in range(4) for r in range(4)]
    del places[LEVEL - HEAD_STEPS]
    return {place: HEAD_STEPS + n for n, place in enumerate(places[:STEPS - HEAD_STEPS])}


SLOTS = bisection_slots()
RANK_SLOT = ("mlp_out", 1, 1)
LN1_SLOT = ("mlp_out", 3, 1)
ADA_STEP = 8


def places():
    place = {}
    for q in range(QUAD):
        for j in range(2):
            place[v_half(q, j)] = (0, j)
    for h in range(H):
        place[qk_half(h)] = (1, h % 2)
    for unit in range(NUNIT):
        for j in range(2):
            place[unit_half(unit, j)] = (unit % 2, j)
    return place


def v_half(q, j):
    return j if q == 0 else 4 + 6 * (q - 1) + j


def qk_half(h):
    if h < 2:
        return 2 + h
    if h < 14:
        return 4 + 6 * ((h - 2) // 4) + 2 + (h - 2) % 4
    return 24 + h - 14


def unit_half(unit, j):
    return 22 + j if unit == 0 else NQKV + 2 * unit + j


PLACE = places()


def block_kernel(nc, x, cond, weights, ada_w, cols, out):
    ctx = ExitStack()
    with ctx:
        here = [(nc.sbuf_base + 31) // 32 * 32]

        def at(name, shape, dt, offset):
            return nc.alloc_sbuf_tensor_at(name, shape, dt, offset=offset)

        def room(nbytes):
            offset = here[0]
            here[0] += (nbytes + 31) // 32 * 32
            assert here[0] <= nc.sbuf_usable_end, here[0]
            return offset

        def new(name, shape, dt):
            n = 4 if dt in (F32, F32R, I32) else 2
            for s in shape[1:]:
                n *= s
            return at(name, shape, dt, room(n))

        xm = new("xm", [P, NT, D], F32)
        adj = new("adj", [P, NT, D], F32)
        rank = adj[:, :, :].rearrange("p i d -> p (i d)")
        keys = rank.bitcast(I32)
        keys16 = rank.bitcast(U16).rearrange("p (n s) -> p n s", s=2)
        xT = new("xT", [P, 2, C, T], F32R)
        wraw = new("wraw", [P, 2, HALF], F32)
        w = new("w", [P, 2, 2, 2 * HALF], F32R)
        qk = new("qk", [P, 2, 2, T], F32R)
        act_at = room(2 * KC * T * 4)
        act = at("act", [P, 2, KC, T], F32R, act_at)
        adaw = at("adaw", [P, C, 6 * D], F32, act_at)
        prob_at = room(NT * T * 4)
        prob = at("prob", [P, NT, T], F32, prob_at)
        xr = at("xr", [P, NT, D], F32, prob_at)
        pt_at = room(2 * NT * T * 4)
        probT = at("probT", [P, 2, NT, T], F32R, pt_at)
        low = at("low", [P, NT * T], F32, pt_at)
        eqm = at("eqm", [P, NT * T], BF16, pt_at + NT * T * 4)
        gtm = at("gtm", [P, NT * T], BF16, pt_at + NT * T * 6)
        v_at = room(2 * 2 * NT * T * 4)
        v = at("v", [P, 2, 2, NT, QUAD * DH], F32R, v_at)
        yT = at("yT", [P, C, T], F32, v_at)
        z = at("z", [P, NT, D], F32, v_at + 8192)
        x2 = at("x2", [P, NT, D], F32, v_at + 16384)
        tmp = at("tmp", [P, 4, T], F32, v_at + 24576)
        tb = new("tb", [P, T], F32)
        flip = tb[:, :].bitcast(I32)
        passed_v = tb[:, :].bitcast(BF16)
        passed_s = new("passed_s", [P, NCOUNT], BF16)
        small = new("small", [P, NCOLS], F32)
        ident = new("ident", [P, P], F32)
        ones = new("ones", [P, P], F16)
        minus_half = new("minus_half", [P, P], F16)
        before = new("before", [P, P], F16)
        ada = new("ada", [P, 6 * C, B], F32)
        ada1 = new("ada1", [P, 2 * C], F32)
        ada2 = new("ada2", [P, 4 * C], F32)
        scur = new("scur", [P, NT], F32)
        rowmax = new("rowmax", [P, NT], F32)
        nbias = new("nbias", [P, NT], F32)
        nxmax = new("nxmax", [P, NT], F32)
        nxsum = new("nxsum", [P, NT], F32)
        rowsum = new("rowsum", [P, NT], F32)
        rinv = new("rinv", [P, NT], F32)
        stats = new("stats", [P, NT, 2, 6], F32)
        meanvar = new("meanvar", [P, NT, 2], F32)
        var = new("var", [P, NT], F32)
        std = new("std", [P, NT], F32)
        rstd = new("rstd", [P, NT], F32)
        newt = new("newt", [P, NT], F32)
        cand = new("cand", [P, 1], F32)
        step_up = new("step_up", [P, 1], F32)
        cnt_v = new("cnt_v", [P, 1], F16)
        cnt_s = new("cnt_s", [P, 1], F16)
        n_gt = new("n_gt", [P, 1], F16)
        n_eq = new("n_eq", [P, 1], F16)
        need = new("need", [P, 1], F32)
        table = new("table", [P, 1], F32)
        rank0 = new("rank0", [P, 1], F32)

        def col(name, i):
            return small[:, COLS[name][0] + i:COLS[name][0] + i + 1]

        bank = [ctx.enter_context(nc.psum_tensor(f"bank{i}", [P, 512], F32)) for i in range(8)]

        def total(step):
            return bank[6 if step < HEAD_STEPS else 3]

        def sem(name):
            return ctx.enter_context(nc.semaphore(name))

        small_in, ada_in, xn_in, tb_in = sem("small_in"), sem("ada_in"), sem("xn_in"), sem("tb_in")
        xr_in = sem("xr_in")
        raw_in = [sem("raw_in0"), sem("raw_in1")]
        ident_zero, consts_ready = sem("ident_zero"), sem("consts_ready")
        w_hi, w_ready = sem("w_hi"), sem("w_ready")
        ada_done = sem("ada_done")
        q_done, k_done, v_done, pv_done = sem("q_done"), sem("k_done"), sem("v_done"), sem("pv_done")
        q_hi, k_hi, v_hi, o_hi = sem("q_hi"), sem("k_hi"), sem("v_hi"), sem("o_hi")
        q_lo, k_lo, v_lo, o_lo = sem("q_lo"), sem("k_lo"), sem("v_lo"), sem("o_lo")
        scores, nbias_ready, exp_done, prob_ready = (sem("scores"), sem("nbias_ready"),
                                                     sem("exp_done"), sem("prob_ready"))
        pt_done, pt_hi, pt_lo = sem("pt_done"), sem("pt_hi"), sem("pt_lo")
        y_done, y_gated, y_back = sem("y_done"), sem("y_gated"), sem("y_back")
        var_ready, std_ready, z_ready = sem("var_ready"), sem("std_ready"), sem("z_ready")
        zt_done, xt_full, xt_hi, xt_lo = sem("zt_done"), sem("xt_full"), sem("xt_hi"), sem("xt_lo")
        f_done, g_done, h_hi, h_lo = sem("f_done"), sem("g_done"), sem("h_hi"), sem("h_lo")
        y2_done, y2_gated, y2_back, out_ready = (sem("y2_done"), sem("y2_gated"), sem("y2_back"),
                                                 sem("out_ready"))
        xmax_ready, xexp_done, adj_ready, diag_done = (sem("xmax_ready"), sem("xexp_done"),
                                                       sem("adj_ready"), sem("diag_done"))
        cand_ready, counted_v, counted_s, total_ready = (sem("cand_ready"), sem("counted_v"),
                                                         sem("counted_s"), sem("total_ready"))
        ties_counted, ranks_ready, xm_ready = sem("ties_counted"), sem("ranks_ready"), sem("xm_ready")
        x_gt_ready = sem("x_gt_ready")
        y_added, y2_added = sem("y_added"), sem("y2_added")
        out_stored = sem("out_stored")
        waits_met = sem("waits_met")

        W_CREDIT = 2
        STORE_CREDIT = 16
        Y2_CREDIT = C

        block = ctx.enter_context(nc.Block())

        x_seq = x.rearrange("b (p i) d -> b p (i d)", p=P)
        out_seq = out.rearrange("b (p i) d -> b p (i d)", p=P)

        def seq(view, b):
            return view[b] if isinstance(b, int) else view[bass.ds(b, 1)].rearrange("a p n -> (a p) n")

        def wait_apart(eng, signal, value):
            eng.wait_ge(signal, value)
            eng.sem_inc(waits_met, 1)

        def w_wait(eng, b, n):
            eng.wait_ge(w_ready, b * NHALF + (n + 1 + W_CREDIT))

        @block.sync
        def _(sp):
            pairs = weights.rearrange("(m s) p n -> m s p n", s=2)

            def load_halves(b, lo, hi):
                with sp.Fori(lo // 2, hi // 2) as m:
                    for slot in range(2):
                        wait_apart(sp, w_ready, b * NHALF + m * 2 + (slot + W_CREDIT - 1))
                        src = pairs[bass.ds(m, 1), slot].rearrange("a p n -> (a p) n")
                        sp.dma_start(wraw[:, slot, :], src).then_inc(raw_in[slot], 16)

            def load_x(b):
                sp.dma_start(rank, seq(x_seq, b)).then_inc(xn_in, 16)
                row = cond[b:b + 1, :] if isinstance(b, int) else cond[bass.ds(b, 1), :]
                sp.dma_start(tb[:, :], row.to_broadcast([P, T])).then_inc(tb_in, 16)

            def load_x_again(b):
                sp.dma_start(xr[:, :, :].rearrange("p i d -> p (i d)"), seq(x_seq, b)).then_inc(xr_in, 16)

            def store(b):
                wait_apart(sp, out_ready, b + 1)
                sp.dma_start(seq(out_seq, b), x2[:, :, :].rearrange("p i d -> p (i d)"))\
                    .then_inc(out_stored, 16)

            def sequence(b, first=False, last=False):
                load_halves(b, 0, 4)
                if not first:
                    store(b - 1)
                if not last:
                    wait_apart(sp, xm_ready, b + 1)
                    load_x(b + 1)
                load_halves(b, 4, NQKV + 6)
                if not last:
                    wait_apart(sp, pt_done, b * (H * NT) + H * NT)
                    load_x_again(b + 1)
                load_halves(b, NQKV + 6, NHALF)

            sp.sem_inc(out_stored, STORE_CREDIT)
            sp.dma_start(small[:, :], cols).then_inc(small_in, 16)
            load_x(0)
            for c in range(C):
                sp.dma_start(adaw[:, c, :], ada_w[c * P:(c + 1) * P, :]).then_inc(ada_in, 16)
            load_x_again(0)
            sequence(0, first=True)
            with sp.Fori(1, B - 1) as b:
                sequence(b)
            sequence(B - 1, last=True)
            store(B - 1)
            sp.wait_ge(out_stored, 16 * B + STORE_CREDIT)

        @block.gpsimd
        def _(pool):
            minus_inf = pool.to_reg(float("-inf"))
            nc.gpsimd.memset(ident[:, :], 0.0).then_inc(ident_zero, 1)
            nc.gpsimd.memset(ones[:, :], 1.0).then_inc(ident_zero, 1)
            nc.gpsimd.memset(minus_half[:, :], -0.5).then_inc(consts_ready, 1)
            pool.wait_ge(ident_zero, 2)
            nc.gpsimd.affine_select(out=ident[:, :], in_=ident[:, :], compare_op=ALU.not_equal, fill=1.0,
                                    base=0, pattern=[[-1, P]], channel_multiplier=1).then_inc(consts_ready, 1)
            nc.gpsimd.affine_select(out=before[:, :], in_=ones[:, :], compare_op=ALU.is_gt, fill=0.0,
                                    base=0, pattern=[[1, P]], channel_multiplier=-1).then_inc(consts_ready, 1)
            pool.sem_inc(w_ready, W_CREDIT)

            def clear_diagonal(t):
                wait_apart(pool, adj_ready, t + 1)
                nc.gpsimd.affine_select(out=adj[:, :, :], in_=adj[:, :, :], compare_op=ALU.not_equal,
                                        fill=minus_inf, base=0, pattern=[[-1, NT], [1, T]],
                                        channel_multiplier=-NT).then_inc(diag_done, 1)

            def split_lo(b, n):
                region, half = PLACE[n]
                span = slice(half * HALF, (half + 1) * HALF)
                pool.wait_ge(w_hi, b * NHALF + (n + 1))
                nc.gpsimd.tensor_tensor(w[:, region, 1, span], wraw[:, n % 2, :],
                                        w[:, region, 0, span].bitcast(F32), ALU.subtract)\
                    .then_inc(w_ready, 1)

            def add_greater(t):
                pool.wait_ge(xr_in, t * 16 + 16)
                x_rows = xr[:, :, :].rearrange("p i d -> p (i d)")
                pool.wait_ge(ties_counted, t + 1)
                nc.gpsimd.tensor_tensor(x_rows, x_rows, gtm[:, :], ALU.add).then_inc(x_gt_ready, 1)

            def sequence(b, last=False):
                for n in range(NHALF):
                    if n == unit_half(NUNIT - 1, 0) and not last:
                        add_greater(b + 1)
                    if n == qk_half(5) and not last:
                        clear_diagonal(b + 1)
                    split_lo(b, n)

            clear_diagonal(0)
            add_greater(0)
            with pool.Fori(0, B - 1) as b:
                sequence(b)
            sequence(B - 1, last=True)

        @block.scalar
        def _(act_e):
            def topk_exp(t):
                for i in range(NT):
                    act_e.wait_ge(xmax_ready, t * NT + (i + 1))
                    ins = nc.scalar.activation(adj[:, i, :], adj[:, i, :], ACT.Exp, bias=nxmax[:, i:i + 1],
                                               accum_out=nxsum[:, i:i + 1])
                ins.then_inc(xexp_done, 1)

            def topk_count(t, step):
                src = keys16[:, NCOUNT:, 1] if step < LEVEL else low[:, NCOUNT:]
                act_e.wait_ge(cand_ready, t * STEPS + (step + 1))
                with nc.allow_low_precision(reason=EXACT):
                    nc.scalar.activation(passed_s[:, :], src, ACT.Sign, bias=cand[:, :], scale=-1.0,
                                         accum_out=cnt_s[:, :]).then_inc(counted_s, 1)

            def ln_root(k, lo=0, hi=NT):
                act_e.wait_ge(var_ready, k + 1)
                nc.scalar.activation(std[:, lo:hi], var[:, lo:hi], ACT.Sqrt).then_inc(std_ready, 1)

            def ln_hi(k, shift, scale1, rows=slice(0, T)):
                for c in range(C):
                    act_e.wait_ge(zt_done, k * C + (c + 1))
                    nc.scalar.activation(tmp[:, c, rows], bank[c][:, rows], ACT.Identity,
                                         bias=shift[:, c:c + 1], scale=scale1[:, c:c + 1]).then_inc(xt_full, 1)
                    nc.scalar.activation(xT[:, 0, c, rows], bank[c][:, rows], ACT.Identity,
                                         bias=shift[:, c:c + 1], scale=scale1[:, c:c + 1]).then_inc(xt_hi, 1)

            def split_hi(b, n, freed, count):
                region, half = PLACE[n]
                act_e.wait_ge(freed, count)
                act_e.wait_ge(raw_in[n % 2], b * (16 * NHALF // 2) + 16 * (n // 2 + 1))
                nc.scalar.copy(w[:, region, 0, half * HALF:(half + 1) * HALF], wraw[:, n % 2, :])\
                    .then_inc(w_hi, 1)

            def split_v(b, q, *halves_of_it):
                for j in halves_of_it or (0, 1):
                    if q:
                        split_hi(b, v_half(q, j), v_done, b * H + QUAD * q)
                    else:
                        split_hi(b, v_half(q, j), y2_done, b * C + (Y2_CREDIT - 1))

            def split_qk(b, h):
                if h >= 2:
                    split_hi(b, qk_half(h), k_done, b * H + (h - 1))
                else:
                    split_hi(b, qk_half(h), y2_done, b * C + Y2_CREDIT)

            def split_unit(b, u, *halves_of_it):
                for half in halves_of_it or (0, 1):
                    n = unit_half(u, half)
                    if u == 0:
                        split_hi(b, n, v_done, b * H + H)
                    elif u == 1:
                        split_hi(b, n, k_done, b * H + H)
                    elif u < 6:
                        split_hi(b, n, y_done, b * Y_PIECES + (u - 1 if u < 5 else Y_PIECES))
                    elif u < 10:
                        split_hi(b, n, f_done, b * KC + 4 * (u - 5))
                    else:
                        split_hi(b, n, y2_done, b * C + (Y2_CREDIT + u - 9))

            def v_part(b, idx):
                act_e.wait_ge(v_done, b * H + (idx + 1))
                if idx == QUAD:
                    act_e.wait_ge(out_stored, b * 16 + STORE_CREDIT)
                bk = bank[4 + idx] if idx < 4 else bank[7]
                nc.scalar.copy(v[:, (idx // 4) % 2, 0, idx % 4, :], bk[:, :]).then_inc(v_hi, 1)

            def qk_part(b, h):
                act_e.wait_ge(q_done, b * H + (h + 1))
                nc.scalar.activation(qk[:, 0, 0, :], bank[4 if h else 1][:, :], ACT.Identity,
                                     bias=col("bq", h))\
                    .then_inc(q_hi, 1)
                act_e.wait_ge(k_done, b * H + (h + 1))
                nc.scalar.activation(qk[:, 1, 0, :], bank[5 if h else 2][:, :], ACT.Identity,
                                     bias=col("bk", h))\
                    .then_inc(k_hi, 1)

            def head(b, h, last):
                for i in range(NT):
                    if h == 0 and i == 1:
                        split_v(b, 1, 1)
                    act_e.wait_ge(nbias_ready, b * (H * NT) + (h * NT + i + 1))
                    nc.scalar.activation(prob[:, i, :], bank[i][:, :], ACT.Exp, bias=nbias[:, i:i + 1],
                                         scale=SCALE, accum_out=rowsum[:, i:i + 1]).then_inc(exp_done, 1)
                if h + 1 < H:
                    qk_part(b, h + 1)
                if h + 2 < H:
                    split_qk(b, h + 2)
                else:
                    split_unit(b, 1, h - (H - 2))
                for j in range(NT):
                    act_e.wait_ge(pt_done, b * (H * NT) + (h * NT + j + 1))
                    nc.scalar.copy(probT[:, 0, j, :], bank[j][:, :]).then_inc(pt_hi, 1)
                if FIRST_TOTAL <= h + 1 and not last:
                    topk_count(b + 1, h + 1 - FIRST_TOTAL)
                if h + QUAD < H:
                    v_part(b, h + QUAD)
                if h == 0 and not last:
                    topk_exp(b + 1)
                refill(b, h, 0)
                act_e.wait_ge(pv_done, b * H + (h + 1))
                nc.scalar.activation(act[:, 0, h, :], bank[6][:, :], ACT.Identity, bias=col("bv", h))\
                    .then_inc(o_hi, 1)
                refill(b, h, 1)

            def refill(b, h, half):
                if h in (3, 7):
                    split_v(b, h // QUAD + 2, half)
                elif h == 11:
                    split_unit(b, 0, half)

            def sequence(b, last=False):
                split_qk(b, 0)
                split_qk(b, 1)
                for idx in range(3):
                    v_part(b, idx)
                qk_part(b, 0)
                nc.scalar.activation(table[:, :], ident[:, 0:1], ACT.Exp)
                split_v(b, 1, 0)
                v_part(b, 3)
                for h in range(H):
                    head(b, h, last)

                def next_count(place):
                    step = SLOTS.get(place)
                    if not last and step is not None and step + 1 < STEPS:
                        topk_count(b + 1, step + 1)

                split_unit(b, 2, 0)
                next_count(("out", 1, 2))
                next_count(("out", 1, 3))
                split_unit(b, 2, 1)
                for r in range(4):
                    if r % 2 == 0:
                        split_unit(b, 3, r // 2)
                    next_count(("out", 2, r))
                split_unit(b, 4)
                ln_root(b * LNS + 1, 0, NT // 2)
                ln_hi(b * LNS + 1, ada2[:, C:2 * C], ada2[:, 2 * C:3 * C], ROWS[0])
                split_unit(b, 5, 0)
                ln_root(b * LNS + 2, NT // 2, NT)
                ln_hi(b * LNS + 2, ada2[:, C:2 * C], ada2[:, 2 * C:3 * C], ROWS[1])
                split_unit(b, 5, 1)
                for f in range(KC):
                    next_count(("mlp_in", f // 4, f % 4))
                    act_e.wait_ge(f_done, b * KC + (f + 1))
                    if f >= 4:
                        act_e.wait_ge(h_lo, b * KC + (f - 3))
                    nc.scalar.activation(tmp[:, f % 4, :], bank[4 + f % 4][:, :], ACT.Gelu,
                                         bias=col("b1", f)).then_inc(g_done, 1)
                    nc.scalar.activation(act[:, 0, f, :], bank[4 + f % 4][:, :], ACT.Gelu,
                                         bias=col("b1", f)).then_inc(h_hi, 1)
                    if f % 4 == 3:
                        split_unit(b, 6 + f // 4, 0)
                    elif f % 4 == 1 and f > 4:
                        split_unit(b, 5 + f // 4, 1)
                for u in range(4):
                    for r in range(4):
                        next_count(("mlp_out", u, r))
                        if r == 1 and u < 3:
                            split_unit(b, 9 + u, 1)
                        elif r == 3 and u < 2:
                            split_unit(b, 10 + u, 0)
                            if u == 1 and not last:
                                ln_root(b * LNS + LNS)
                        elif not last and (u, r) in ((2, 3), (3, 1)):
                            split_v(b + 1, 0, u - 2)
                if not last:
                    ln_hi(b * LNS + LNS, ada1[:, 0:C], ada1[:, C:2 * C])

            act_e.wait_ge(small_in, 16)
            act_e.wait_ge(consts_ready, 3)
            topk_exp(0)
            for step in range(STEPS):
                topk_count(0, step)
            split_v(0, 0)
            ln_root(0)
            ln_hi(0, ada1[:, 0:C], ada1[:, C:2 * C])
            with act_e.Fori(0, B - 1) as b:
                sequence(b)
            sequence(B - 1, last=True)

        @block.vector
        def _(dve):
            V = nc.vector

            def count(t, step):
                src = keys16[:, :NCOUNT, 1] if step < LEVEL else low[:, :NCOUNT]
                with nc.allow_low_precision(reason=EXACT):
                    V.tensor_scalar(passed_v, src, cand[:, :], None, op0=ALU.is_ge, op1=ALU.add,
                                    accum_out=cnt_v[:, :]).then_inc(counted_v, 1)

            def start_level(t, step):
                V.memset(cand[:, :], TOP_BIT - 0.5).then_inc(cand_ready, 1)
                dve.drain()
                count(t, step)

            def topk_rowmax(t):
                dve.wait_ge(xn_in, t * 16 + 16)
                for i in range(NT):
                    V.tensor_reduce(nxmax[:, i:i + 1], adj[:, i, :], AX.X, ALU.max, negate=True)\
                        .then_inc(xmax_ready, 1)
                if isinstance(t, int):
                    dve.wait_ge(small_in, 16)
                src = small[:, COLS["s"][0]:COLS["s"][1]].rearrange("p (b i) -> p b i", b=B)
                V.tensor_copy(scur[:, :], src[:, t, :] if isinstance(t, int) else
                              src[:, bass.ds(t, 1), :].rearrange("p a i -> p (a i)"))

            def topk_softmax(t):
                dve.wait_ge(xexp_done, t + 1)
                V.reciprocal(rinv[:, :], nxsum[:, :])
                dve.drain()
                for i in range(NT):
                    V.tensor_scalar(adj[:, i, :], adj[:, i, :], rinv[:, i:i + 1], float(np.float32(T ** -0.5)),
                                    ALU.mult, ALU.mult)

            def topk_adj(t):
                dve.drain()
                dve.wait_ge(tb_in, t * 16 + 16)
                for i in range(NT):
                    ins = V.scalar_tensor_tensor(adj[:, i, :], tb[:, :], scur[:, i:i + 1], adj[:, i, :],
                                                 ALU.mult, ALU.mult)
                ins.then_inc(adj_ready, 1)

            def topk_keys(t, lo, hi):
                if lo == 0:
                    dve.wait_ge(diag_done, t + 1)
                for i in range(lo, hi):
                    part = keys[:, i * T:(i + 1) * T]
                    V.tensor_scalar(flip, part, 31, -(1 << 31), ALU.arith_shift_right, ALU.bitwise_or)
                    dve.drain()
                    V.tensor_tensor(part, part, flip, ALU.bitwise_xor)
                    dve.drain()

            def topk_step(t, step):
                topk_move(t, step)
                if step % LEVEL != LEVEL - 1:
                    count(t, step + 1)

            def topk_move(t, step):
                dve.wait_ge(total_ready, t * STEPS + (step + 1))
                bit = TOP_BIT / (1 << step % LEVEL)
                V.tensor_scalar(step_up[:, :], total(step)[:, 0:1], float(KTOP - P * NCOUNT // 2) - 0.5, bit,
                                ALU.is_gt, ALU.mult)
                dve.drain()
                move = V.scalar_tensor_tensor(cand[:, :], step_up[:, :], -bit / 2, cand[:, :], ALU.add, ALU.add)
                if step % LEVEL != LEVEL - 1:
                    move.then_inc(cand_ready, 1)
                dve.drain()
                if step == LEVEL - 1:
                    V.tensor_scalar(low[:, :], keys16[:, :, 1], cand[:, :], float(1 << 17),
                                    ALU.subtract, ALU.mult)
                    dve.drain()
                    V.tensor_tensor(low[:, :], low[:, :], keys16[:, :, 0], ALU.add)
                    dve.drain()
                    start_level(t, step + 1)
                elif step == STEPS - 1:
                    with nc.allow_low_precision(reason=EXACT):
                        V.tensor_scalar(eqm[:, :], low[:, :], cand[:, :], None, op0=ALU.is_equal, op1=ALU.add,
                                        accum_out=n_eq[:, :])
                        V.tensor_scalar(gtm[:, :], low[:, :], cand[:, :], None, op0=ALU.is_gt, op1=ALU.add,
                                        accum_out=n_gt[:, :]).then_inc(ties_counted, 1)

            def topk_mask(t):
                dve.wait_ge(ranks_ready, t + 1)
                V.tensor_scalar(need[:, :], bank[3][:, 0:1], -1.0, float(KTOP), ALU.mult, ALU.add)
                V.tensor_copy(rank0[:, :], bank[3][:, 1:2])
                dve.drain()
                V.tensor_tensor_scan(rank, eqm[:, :], eqm[:, :], rank0[:, :], ALU.add, ALU.max)
                dve.drain()
                V.scalar_tensor_tensor(eqm[:, :], rank, need[:, :], eqm[:, :], ALU.is_le, ALU.mult)
                dve.drain()
                dve.wait_ge(x_gt_ready, t + 1)
                V.tensor_tensor(xm[:, :, :].rearrange("p i d -> p (i d)"),
                                xr[:, :, :].rearrange("p i d -> p (i d)"), eqm[:, :], ALU.add)\
                    .then_inc(xm_ready, 1)
                dve.drain()

            def row_stats(src, part, lo, hi, tiles=range(NT)):
                for i in tiles:
                    V.bn_stats(stats[:, i, part, :], src[:, i, lo:hi])

            def normalise(k, src, parts, lo=0, hi=NT):
                dve.drain()
                for i in range(lo, hi):
                    V.bn_aggr(meanvar[:, i, :], stats[:, i, 0:parts, :].rearrange("p a s -> p (a s)"))
                dve.drain()
                V.tensor_scalar(var[:, lo:hi], meanvar[:, lo:hi, 1], EPS, None, ALU.add).then_inc(var_ready, 1)
                dve.wait_ge(std_ready, k + 1)
                V.reciprocal(rstd[:, lo:hi], std[:, lo:hi])
                dve.drain()
                V.tensor_tensor(newt[:, lo:hi], rstd[:, lo:hi], rstd[:, lo:hi], ALU.mult)
                dve.drain()
                V.scalar_tensor_tensor(newt[:, lo:hi], newt[:, lo:hi], -0.5, var[:, lo:hi], ALU.mult, ALU.mult)
                dve.drain()
                V.scalar_tensor_tensor(rstd[:, lo:hi], newt[:, lo:hi], 1.5, rstd[:, lo:hi], ALU.add, ALU.mult)
                dve.drain()
                for i in range(lo, hi):
                    V.tensor_scalar(z[:, i, :], src[:, i, :], meanvar[:, i, 0:1], rstd[:, i:i + 1],
                                    ALU.subtract, ALU.mult).then_inc(z_ready, 1)

            def modulate_lo(k, rows=slice(0, T)):
                for c in range(C):
                    dve.wait_ge(xt_full, k * C + (c + 1))
                    dve.wait_ge(xt_hi, k * C + (c + 1))
                    V.tensor_tensor(xT[:, 1, c, rows], tmp[:, c, rows], xT[:, 0, c, rows].bitcast(F32),
                                    ALU.subtract).then_inc(xt_lo, 1)

            def v_part(b, idx):
                dve.wait_ge(v_hi, b * H + (idx + 1))
                bk = bank[4 + idx] if idx < 4 else bank[7]
                V.tensor_tensor(v[:, (idx // 4) % 2, 1, idx % 4, :], bk[:, :],
                                v[:, (idx // 4) % 2, 0, idx % 4, :].bitcast(F32), ALU.subtract).then_inc(v_lo, 1)

            def biased_lo(dst, src, bias, hi):
                return V.scalar_tensor_tensor(dst, src, bias, hi.bitcast(F32), ALU.add, ALU.subtract)

            def qk_part(b, h):
                dve.wait_ge(q_hi, b * H + (h + 1))
                biased_lo(qk[:, 0, 1, :], bank[4 if h else 1][:, :], col("bq", h), qk[:, 0, 0, :]).then_inc(q_lo, 1)
                dve.wait_ge(k_hi, b * H + (h + 1))
                biased_lo(qk[:, 1, 1, :], bank[5 if h else 2][:, :], col("bk", h), qk[:, 1, 0, :]).then_inc(k_lo, 1)

            def topk_under_head(t, h):
                if h == 0:
                    topk_rowmax(t)
                elif h == 1:
                    topk_softmax(t)
                elif h == 2:
                    topk_adj(t)
                elif h == 3:
                    topk_keys(t, 0, 3)
                elif h == 4:
                    topk_keys(t, 3, NT)
                    start_level(t, 0)
                elif h >= FIRST_TOTAL:
                    count(t, h + 1 - FIRST_TOTAL)

            def head(b, h, last):
                tile = h * NT
                for i in range(NT + 1):
                    if i < NT:
                        dve.wait_ge(scores, b * (H * NT) + (tile + i + 1))
                        V.reduce_max(rowmax[:, i:i + 1], bank[i][:, :], AX.X)
                    if i:
                        dve.wait_ge(exp_done, b * (H * NT) + (tile + i))
                        V.reciprocal(rinv[:, i - 1:i], rowsum[:, i - 1:i])
                    dve.drain()
                    if i < NT:
                        V.tensor_scalar(nbias[:, i:i + 1], rowmax[:, i:i + 1], -SCALE, None, ALU.mult)\
                            .then_inc(nbias_ready, 1)
                    if i:
                        V.tensor_scalar(prob[:, i - 1, :], prob[:, i - 1, :], rinv[:, i - 1:i], None, ALU.mult)\
                            .then_inc(prob_ready, 1)
                if FIRST_TOTAL <= h and not last:
                    topk_move(b + 1, h - FIRST_TOTAL)
                if h + 1 < H:
                    qk_part(b, h + 1)
                for j in range(NT):
                    dve.wait_ge(pt_hi, b * (H * NT) + (tile + j + 1))
                    V.tensor_tensor(probT[:, 1, j, :], bank[j][:, :], probT[:, 0, j, :].bitcast(F32),
                                    ALU.subtract).then_inc(pt_lo, 1)
                if not last:
                    topk_under_head(b + 1, h)
                if h + QUAD < H:
                    v_part(b, h + QUAD)
                dve.wait_ge(o_hi, b * H + (h + 1))
                biased_lo(act[:, 1, h, :], bank[6][:, :], col("bv", h), act[:, 0, h, :]).then_inc(o_lo, 1)

            def gate(gated, u, bias, gates, bk, rows=slice(0, T)):
                V.tensor_scalar(yT[:, u, rows], bk[:, rows], col(bias, u), gates[:, u:u + 1],
                                ALU.add, ALU.mult).then_inc(gated, 1)

            def hidden_lo(b, f):
                dve.wait_ge(h_hi, b * KC + (f + 1))
                V.tensor_tensor(act[:, 1, f, :], tmp[:, f % 4, :], act[:, 0, f, :].bitcast(F32),
                                ALU.subtract).then_inc(h_lo, 1)

            def sequence(b, last=False):
                src = ada[:, 2 * C:6 * C, b] if isinstance(b, int) else \
                    ada[:, 2 * C:6 * C, bass.ds(b, 1)].rearrange("p c a -> p (c a)")
                V.tensor_copy(ada2[:, :], src)
                for idx in range(3):
                    v_part(b, idx)
                qk_part(b, 0)
                v_part(b, 3)
                for h in range(H):
                    head(b, h, last)

                def step_at(place):
                    if not last and place in SLOTS:
                        topk_step(b + 1, SLOTS[place])

                def attn_gate(u, half=0):
                    dve.wait_ge(y_done, b * Y_PIECES + (u + 1 + half))
                    gate(y_gated, u, "ob", ada2[:, 0:C], bank[BANKS["out"][u + half]],
                         ROWS[half] if u == C - 1 else slice(0, T))

                def mlp_gate(u):
                    dve.wait_ge(y2_done, b * C + (u + 1 + Y2_CREDIT))
                    gate(y2_gated, u, "b2", ada2[:, 3 * C:4 * C], bank[BANKS["mlp_out"][u]])

                def add_back(u, base, lo=0, hi=NT):
                    part = slice(u * P, (u + 1) * P)
                    return V.tensor_tensor(x2[:, lo:hi, part], base[:, lo:hi, part],
                                           bank[u][:, lo * P:hi * P].rearrange("p (i j) -> p i j", i=hi - lo),
                                           ALU.add)

                def attn_add(u, half=0):
                    dve.wait_ge(y_back, b * Y_PIECES + (u + 1 + half))
                    if u < C - 1:
                        return add_back(u, xm)
                    return add_back(u, xm, half * NT // 2, (half + 1) * NT // 2)

                def mlp_add(u):
                    dve.wait_ge(y2_back, b * C + (u + 1))
                    return add_back(u, x2)

                step_at(("out", 1, 2))
                attn_gate(0)
                step_at(("out", 1, 3))
                attn_gate(1)
                for r in range(4):
                    step_at(("out", 2, r))
                    if r in (1, 2):
                        attn_add(r - 1)
                attn_gate(2)
                attn_gate(3, 0)
                attn_add(2)
                attn_add(3, 0)
                dve.drain()
                row_stats(x2, 0, 0, D, range(0, NT // 2))
                normalise(b * LNS + 1, x2, 1, 0, NT // 2)
                attn_gate(3, 1)
                attn_add(3, 1).then_inc(y_added, 1)
                dve.drain()
                row_stats(x2, 0, 0, D, range(NT // 2, NT))
                modulate_lo(b * LNS + 1, ROWS[0])
                normalise(b * LNS + 2, x2, 1, NT // 2, NT)
                modulate_lo(b * LNS + 2, ROWS[1])
                V.tensor_tensor(x2[:, :, :].rearrange("p i d -> p (i d)"),
                                x2[:, :, :].rearrange("p i d -> p (i d)"),
                                xm[:, :, :].rearrange("p i d -> p (i d)"), ALU.add)
                for f in range(KC):
                    step_at(("mlp_in", f // 4, f % 4))
                    if f:
                        hidden_lo(b, f - 1)
                hidden_lo(b, KC - 1)
                for u in range(4):
                    for r in range(4):
                        if u and r == 0:
                            mlp_gate(u - 1)
                        step_at(("mlp_out", u, r))
                        if (u, r) == (1, 2):
                            mlp_add(0)
                        if u == 3 and r == 0:
                            mlp_add(1)
                            mlp_add(2).then_inc(y2_added, 1)
                        if not last and ("mlp_out", u, r) == RANK_SLOT:
                            topk_mask(b + 1)
                            next_modulation(b + 1)
                            row_stats(xm, 0, 0, D)
                            normalise(b * LNS + LNS, xm, 1)
                if not last:
                    modulate_lo(b * LNS + LNS)
                mlp_gate(3)
                mlp_add(3).then_inc(out_ready, 1)

            def next_modulation(t):
                src = ada[:, 0:2 * C, t] if isinstance(t, int) else \
                    ada[:, 0:2 * C, bass.ds(t, 1)].rearrange("p c a -> p (c a)")
                V.tensor_copy(ada1[:, :], src)

            topk_rowmax(0)
            topk_softmax(0)
            topk_adj(0)
            topk_keys(0, 0, NT)
            start_level(0, 0)
            for step in range(STEPS):
                topk_step(0, step)
            dve.wait_ge(ada_done, 1)
            ada_b = small[:, COLS["ada_b"][0]:COLS["ada_b"][1]]
            V.tensor_tensor(ada[:, :, :], bank[0][:, 0:6 * C * B].rearrange("p (m b) -> p m b", b=B),
                            ada_b.unsqueeze(2).to_broadcast([P, 6 * C, B]), ALU.add)
            dve.drain()
            for part in (1, 4):
                V.tensor_scalar(ada[:, part * C:(part + 1) * C, :], ada[:, part * C:(part + 1) * C, :],
                                1.0, None, ALU.add)
            dve.drain()
            next_modulation(0)
            topk_mask(0)
            row_stats(xm, 0, 0, D)
            normalise(0, xm, 1)
            modulate_lo(0)
            V.memset(newt[:, :], 0.0).then_inc(o_lo, 1)
            with dve.Fori(0, B - 1) as b:
                sequence(b)
            sequence(B - 1, last=True)

        @block.tensor
        def _(pe):
            def mm3(dst, w_hi_ap, w_lo_ap, x_hi_ap, x_lo_ap, first, last):
                pe.matmul(dst, w_hi_ap, x_hi_ap, start=first, stop=False)
                pe.matmul(dst, w_hi_ap, x_lo_ap, start=False, stop=False)
                return pe.matmul(dst, w_lo_ap, x_hi_ap, start=False, stop=last)

            def take_total(t, step):
                pe.wait_ge(counted_v, t * STEPS + (step + 1))
                pe.wait_ge(counted_s, t * STEPS + (step + 1))
                pe.matmul(total(step)[:, 0:1], ones[:, :], cnt_v[:, :], start=True, stop=False)
                pe.matmul(total(step)[:, 0:1], minus_half[:, :], cnt_s[:, :], start=False, stop=True)\
                    .then_inc(total_ready, 1)

            def take_ranks(t):
                pe.wait_ge(ties_counted, t + 1)
                pe.matmul(bank[3][:, 0:1], ones[:, :], n_gt[:, :], start=True, stop=True)
                pe.matmul(bank[3][:, 1:2], before[:, :], n_eq[:, :], start=True, stop=True)\
                    .then_inc(ranks_ready, 1)

            def transpose_z(k, tiles=range(NT), chunks=range(C)):
                for i in tiles:
                    pe.wait_ge(z_ready, k * NT + (i + 1))
                    for c in chunks:
                        ins = pe.transpose(bank[c][:, i * P:(i + 1) * P], z[:, i, c * P:(c + 1) * P], ident[:, :])
                        if i == tiles[-1]:
                            ins.then_inc(zt_done, 1)

            def v_mm(bk, m, c):
                part, rows = slice(c * T, (c + 1) * T), slice(m * P, (m + 1) * P)
                return mm3(bk[:, :], xT[:, 0, c, rows], xT[:, 1, c, rows], w[:, 0, 0, part], w[:, 0, 1, part],
                           c == 0, c == C - 1)

            def first_v_tiles(b):
                for c in range(C):
                    if c % 2 == 0:
                        w_wait(pe, b, v_half(0, c // 2))
                    pe.wait_ge(xt_lo, b * (LNS * C) + (c + 1))
                    for m in range(NT - 1):
                        ins = v_mm(bank[4 + m], m, c)
                        if c == C - 1:
                            ins.then_inc(v_done, 1)

            def v_tile(b, idx):
                q, m = idx // 4, idx % 4
                if idx >= QUAD:
                    pe.wait_ge(v_lo, b * H + idx)
                for c in range(C):
                    if m == 0 and c % 2 == 0:
                        w_wait(pe, b, v_half(q, c // 2))
                    ins = v_mm(bank[7], m, c)
                ins.then_inc(v_done, 1)

            def qk_proj(b, h):
                w_wait(pe, b, qk_half(h))
                for which, done in ((0, q_done), (1, k_done)):
                    bk = bank[(4 if h else 1) + which]
                    if h == 1:
                        pe.wait_ge(v_lo, b * H + (which + 1))
                    for c in range(C):
                        part = slice((h % 2) * HALF + c * 2 * P + which * P, (h % 2) * HALF + c * 2 * P + which * P + P)
                        ins = mm3(bk[:, :], w[:, 1, 0, part], w[:, 1, 1, part], xT[:, 0, c, :], xT[:, 1, c, :],
                                  c == 0, c == C - 1)
                    ins.then_inc(done, 1)

            def head(b, h, last):
                pe.wait_ge(q_lo, b * H + (h + 1))
                pe.wait_ge(k_lo, b * H + (h + 1))
                for i in range(NT):
                    rows = slice(i * P, (i + 1) * P)
                    mm3(bank[i][:, :], qk[:, 0, 0, rows], qk[:, 0, 1, rows], qk[:, 1, 0, :], qk[:, 1, 1, :],
                        True, True).then_inc(scores, 1)
                step = h - FIRST_TOTAL
                if 0 <= step < HEAD_STEPS and not last:
                    pe.wait_ge(o_lo, b * H + (h + 1))
                    take_total(b + 1, step)
                if h + 1 < H:
                    qk_proj(b, h + 1)
                if h == H - 1:
                    wide(b, "out", 0, 9, KC - 1, y_done)
                    wide(b, "out", 1, 0, 6, y_done)
                pe.wait_ge(prob_ready, b * (H * NT) + (h * NT + NT))
                for j in range(NT):
                    for i in range(NT):
                        ins = pe.transpose(bank[j][:, i * P:(i + 1) * P], prob[:, i, j * P:(j + 1) * P], ident[:, :])
                    ins.then_inc(pt_done, 1)
                if h + QUAD < H:
                    v_tile(b, h + QUAD)
                elif h < H - 1:
                    wide(b, "out", 0, 3 * (h + QUAD - H), 3 * (h + QUAD - H) + 3, y_done)
                else:
                    wide(b, "out", 1, 6, 8, y_done)
                q, m = h // QUAD, h % QUAD
                if m == 0:
                    pe.wait_ge(v_lo, b * H + 4 * (q + 1))
                pe.wait_ge(o_lo, b * H + (h + 1))
                if 0 <= step < HEAD_STEPS and not last:
                    pe.wait_ge(cand_ready, (b + 1) * STEPS + (step + 2))
                for j in range(NT):
                    pe.wait_ge(pt_lo, b * (H * NT) + (h * NT + j + 1))
                    part = slice(m * P, (m + 1) * P)
                    ins = mm3(bank[6][:, :], v[:, q % 2, 0, j, part], v[:, q % 2, 1, j, part],
                              probT[:, 0, j, :], probT[:, 1, j, :], j == 0, j == NT - 1)
                ins.then_inc(pv_done, 1)

            def transpose_back(b, u, gated, back, tiles=range(NT), half=0):
                per = Y_PIECES if gated is y_gated else C
                pe.wait_ge(gated, b * per + (u + 1 + half))
                for i in tiles:
                    ins = pe.transpose(bank[u][:, i * P:(i + 1) * P], yT[:, u, i * P:(i + 1) * P], ident[:, :])
                ins.then_inc(back, 1)

            def wide(b, phase, u, lo, hi, done, rows=slice(0, T), half=0):
                unit = (0 if phase == "out" else 8) + u
                for kc in range(lo, hi):
                    if kc % 8 == 0:
                        w_wait(pe, b, unit_half(unit, kc // 8))
                    if phase == "out" and kc >= KC - 2:
                        pe.wait_ge(o_lo, b * H + (kc + 2))
                    if phase == "mlp_out" and kc == 0:
                        pe.wait_ge(h_hi, b * KC + (KC - 3 + u))
                    if phase == "mlp_out" and u == 0 and (kc % 4 == 0 or kc == KC - 1):
                        pe.wait_ge(h_lo, b * KC + (KC if kc == KC - 1 else min(kc + 4, KC - 1)))
                    part = slice(kc * P, (kc + 1) * P)
                    ins = mm3(bank[BANKS[phase][u + half]][:, rows], w[:, unit % 2, 0, part], w[:, unit % 2, 1, part],
                              act[:, 0, kc, rows], act[:, 1, kc, rows], kc == 0, kc == KC - 1)
                    if kc == KC - 1:
                        ins.then_inc(done, 1)

            def between(b, place, last):
                if last:
                    return
                if place in SLOTS:
                    take_total(b + 1, SLOTS[place])
                if place == RANK_SLOT:
                    take_ranks(b + 1)
                if place == LN1_SLOT:
                    pe.wait_ge(y2_added, b + 1)
                    transpose_z(b * 2 + 2)

            def mlp_in(b, last):
                def mm(f, c, rows=slice(0, T)):
                    unit = 4 + f // 4
                    part = slice(c * T + (f % 4) * P, c * T + (f % 4 + 1) * P)
                    return mm3(bank[4 + f % 4][:, rows], w[:, unit % 2, 0, part], w[:, unit % 2, 1, part],
                               xT[:, 0, c, rows], xT[:, 1, c, rows], c == 0, c == C - 1)

                for half in range(2):
                    if half:
                        transpose_z(b * 2 + 1, range(NT // 2, NT))
                    for c in range(C):
                        if c % 2 == 0:
                            w_wait(pe, b, unit_half(4, c // 2))
                        pe.wait_ge(xt_lo, b * (LNS * C) + ((half + 1) * C + c + 1))
                        for f in range(4):
                            ins = mm(f, c, ROWS[half])
                            if half and c == C - 1:
                                ins.then_inc(f_done, 1)
                between(b, ("mlp_in", 0, 3), last)
                for f in range(4, KC):
                    pe.wait_ge(h_hi, b * KC + (f - 3))
                    for c in range(C):
                        if f % 4 == 0 and c % 2 == 0:
                            w_wait(pe, b, unit_half(4 + f // 4, c // 2))
                        ins = mm(f, c)
                    ins.then_inc(f_done, 1)
                    between(b, ("mlp_in", f // 4, f % 4), last)

            def sequence(b, last=False):
                first_v_tiles(b)
                qk_proj(b, 0)
                v_tile(b, 3)
                for h in range(H):
                    head(b, h, last)
                wide(b, "out", 1, 8, 10, y_done)
                wide(b, "out", 0, KC - 1, KC, y_done)
                between(b, ("out", 1, 2), last)
                wide(b, "out", 1, 10, KC, y_done)
                between(b, ("out", 1, 3), last)
                for r in range(4):
                    wide(b, "out", 2, 4 * r, 4 * r + 4, y_done)
                    if r < 2:
                        transpose_back(b, r, y_gated, y_back)
                    between(b, ("out", 2, r), last)
                wide(b, "out", 3, 0, KC, y_done, ROWS[0])
                transpose_back(b, 2, y_gated, y_back)
                wide(b, "out", 3, 0, 2, y_done, ROWS[1], 1)
                transpose_back(b, 3, y_gated, y_back, range(0, NT // 2))
                wide(b, "out", 3, 2, KC, y_done, ROWS[1], 1)
                transpose_z(b * 2 + 1, range(0, NT // 2), range(0, C - 1))
                transpose_back(b, 3, y_gated, y_back, range(NT // 2, NT), 1)
                pe.wait_ge(y_added, b + 1)
                transpose_z(b * 2 + 1, range(0, NT // 2), range(C - 1, C))
                mlp_in(b, last)
                for u in range(4):
                    for r in range(4):
                        wide(b, "mlp_out", u, 4 * r, 4 * r + 4, y2_done)
                        if (u, r) == (1, 2):
                            transpose_back(b, 0, y2_gated, y2_back)
                        elif (u, r) == (3, 0):
                            transpose_back(b, 1, y2_gated, y2_back)
                            transpose_back(b, 2, y2_gated, y2_back)
                        between(b, ("mlp_out", u, r), last)
                if not last:
                    pe.wait_ge(xt_lo, b * (LNS * C) + (LNS + 1) * C)
                transpose_back(b, 3, y2_gated, y2_back)

            pe.sem_inc(y2_done, Y2_CREDIT)
            pe.wait_ge(consts_ready, 3)
            c0 = COLS["cond"][0]
            for step in range(STEPS):
                take_total(0, step)
                if step == ADA_STEP:
                    pe.wait_ge(small_in, 16)
                    pe.wait_ge(ada_in, 16 * C)
                if step >= ADA_STEP:
                    m = step - ADA_STEP
                    for c in range(C):
                        ins = pe.matmul(bank[0][:, m * B:(m + 1) * B], adaw[:, c, m * P:(m + 1) * P],
                                        small[:, c0 + c * B:c0 + (c + 1) * B], start=c == 0, stop=c == C - 1)
            ins.then_inc(ada_done, 1)
            take_ranks(0)
            transpose_z(0)
            with pe.Fori(0, B - 1) as b:
                sequence(b)
            sequence(B - 1, last=True)


def _half_units(qkv_w, out_w, w1, w2):
    n = H * DH
    q = qkv_w.reshape(C, P, 3 * n)

    def pack(a):
        return a.transpose(1, 0, 2).reshape(P, -1)

    halves = np.empty((NHALF, P, HALF), qkv_w.dtype)
    for h in range(H):
        one = np.concatenate([q[:, :, h * DH:(h + 1) * DH], q[:, :, n + h * DH:n + (h + 1) * DH]], axis=2)
        halves[qk_half(h)] = pack(one)
    for g in range(H // QUAD):
        one = pack(q[:, :, 2 * n + g * QUAD * DH:2 * n + (g + 1) * QUAD * DH])
        halves[v_half(g, 0)], halves[v_half(g, 1)] = one[:, :HALF], one[:, HALF:]
    for u in range(4):
        units = (pack(out_w.reshape(KC, P, D)[:, :, u * P:(u + 1) * P]),
                 pack(w1.reshape(C, P, F)[:, :, u * T:(u + 1) * T]),
                 pack(w2.reshape(KC, P, D)[:, :, u * P:(u + 1) * P]))
        for layer, one in enumerate(units):
            for j in range(2):
                halves[unit_half(4 * layer + u, j)] = one[:, j * HALF:(j + 1) * HALF]
    return halves


def kernel(x, fside_BxSx1_0, cond_2048, L1_cond_ada_w, L1_cond_ada_b, L1_cond_qkv_w, L1_cond_qkv_b,
           L1_cond_out_w, L1_cond_out_b, L1_cond_ffn_w1, L1_cond_ffn_b1, L1_cond_ffn_w2, L1_cond_ffn_b2):
    import concourse.bacc as bacc
    from concourse.bass_utils import run_bass_kernel_spmd

    x, s, cond, ada_w, ada_b, qkv_w, qkv_b, out_w, out_b, w1, b1, w2, b2 = (
        np.asarray(a) for a in (x, fside_BxSx1_0, cond_2048, L1_cond_ada_w, L1_cond_ada_b, L1_cond_qkv_w,
                                L1_cond_qkv_b, L1_cond_out_w, L1_cond_out_b, L1_cond_ffn_w1, L1_cond_ffn_b1,
                                L1_cond_ffn_w2, L1_cond_ffn_b2))

    def columns(a):
        return a.reshape(-1, P).T

    cols = np.concatenate([
        columns(qkv_b), columns(out_b), columns(b1), columns(b2), columns(ada_b),
        s.reshape(B, P, NT).transpose(1, 0, 2).reshape(P, B * NT),
        cond.reshape(B, C, P).transpose(2, 1, 0).reshape(P, C * B)], axis=1)
    arrays = {"x_in": np.ascontiguousarray(x), "cond_in": np.ascontiguousarray(cond),
              "weights_in": _half_units(qkv_w, out_w, w1, w2), "ada_w_in": np.ascontiguousarray(ada_w),
              "cols_in": np.ascontiguousarray(cols)}
    nc = bacc.Bacc("TRN2", target_bir_lowering=False, num_devices=1)
    args = [nc.dram_tensor(name, a.shape, mybir.dt.from_np(a.dtype), kind="ExternalInput").ap()
            for name, a in arrays.items()]
    out = nc.dram_tensor("out", (B, T, D), F32, kind="ExternalOutput").ap()
    block_kernel(nc, *args, out)
    return run_bass_kernel_spmd(nc, [arrays], core_ids=[0]).results[0]["out"]
```
